# Optimizing a Trainium2 kernel written in Bass

```python
import numpy as np
import jax
import jax.numpy as jnp

def _softmax(x, axis=-1):
    return jax.nn.softmax(x, axis=axis)

def _gelu(x):
    return jax.nn.gelu(x, approximate=True)

def _silu(x):
    return jax.nn.silu(x)

def _sigmoid(x):
    return jax.nn.sigmoid(x)

def _layernorm(x, axis=-1, eps=1e-05):
    m = jnp.mean(x, axis=axis, keepdims=True)
    v = jnp.var(x, axis=axis, keepdims=True)
    return (x - m) / jnp.sqrt(v + eps)

def _scatter_add(tgt, idx, src, axis=0):
    return tgt.at[idx].add(src)

def _segment_sum(src, seg, n):
    return jax.ops.segment_sum(src, seg, n)
kernel_name = 'mk_audio_tower_d1_tok_audfeat256_r4_b17c08'

def setup_inputs(seed: int=0):
    np.random.seed(seed)
    _w = jnp.asarray

    def _rec_inputs():
        import jax
        import jax.numpy as jnp
        _rk = jax.random.key(seed)
        x = -0.000520686 + 1.00062 * jax.random.normal(jax.random.fold_in(_rk, 1), (32, 750, 64), jnp.float32)
        return x
    x = _rec_inputs()

    def _L0_tok_setup():
        import jax, jax.numpy as jnp
        import numpy as np
        BATCH = 2
        SEQ = 1024
        D_MODEL = 64
        N_STATE = 64
        DT_RANK = 1
        NUM_LAYERS = 3

        def _ssm_layer(x, A_log, Dp, W_dbc, W_dt, b_dt):
            A = -jnp.exp(A_log)
            dbc = jnp.einsum('ble,ce->blc', x, W_dbc)
            delta, Bm, Cm = jnp.split(dbc, [DT_RANK, DT_RANK + N_STATE], axis=-1)
            delta = jax.nn.softplus(jnp.einsum('blr,er->ble', delta, W_dt) + b_dt)
            dA = jnp.exp(delta[..., None] * A)
            dBx = (delta * x)[..., None] * Bm[:, :, None, :]

            def combine(c1, c2):
                a1, h1 = c1
                a2, h2 = c2
                return (a1 * a2, h1 * a2 + h2)
            _, hs = jax.lax.associative_scan(combine, (dA, dBx), axis=1)
            y = jnp.einsum('blen,bln->ble', hs, Cm)
            return y + Dp * x
        key = jax.random.key(seed)
        kx, kw1, kw2 = jax.random.split(key, 3)
        x = jax.random.normal(kx, (BATCH, SEQ, D_MODEL), dtype=jnp.float32)
        A_log = jnp.broadcast_to(jnp.log(jnp.arange(1, N_STATE + 1, dtype=jnp.float32)), (NUM_LAYERS, D_MODEL, N_STATE)).copy()
        D = jnp.ones((NUM_LAYERS, D_MODEL), dtype=jnp.float32)
        W_dbc = 0.02 * jax.random.normal(kw1, (NUM_LAYERS, DT_RANK + 2 * N_STATE, D_MODEL), dtype=jnp.float32)
        W_dt = 0.02 * jax.random.normal(kw2, (NUM_LAYERS, D_MODEL, DT_RANK), dtype=jnp.float32)
        b_dt = jnp.zeros((NUM_LAYERS, D_MODEL), dtype=jnp.float32)
        return {'x': x, 'A_log': A_log, 'D': D, 'W_dbc': W_dbc, 'W_dt': W_dt, 'b_dt': b_dt}
    _L0_tok_all = _L0_tok_setup()
    _L0_tok_in = {k: v for k, v in _L0_tok_all.items() if k in ('A_log', 'D', 'W_dbc', 'W_dt', 'b_dt')}
    del _L0_tok_all

    def _L0_attn_setup():
        import jax, jax.numpy as jnp
        import numpy as np
        A, Bc, Cc = (0.5, 1.0, 1.0)
        H = 8
        EPS = 1e-12

        def _normalize(t):
            n = jnp.linalg.norm(t, axis=-1, keepdims=True)
            return t / jnp.maximum(n, EPS)
        key = jax.random.key(seed)
        ks = jax.random.split(key, 5)
        B, N, C = (8, 512, 64)
        D = C // H
        x = jax.random.normal(ks[0], (B, N, C), dtype=jnp.float32)
        Wqkv = jax.random.normal(ks[1], (3 * H * D, C), dtype=jnp.float32) * 0.02
        bqkv = jnp.zeros((3 * H * D,), dtype=jnp.float32)
        Wproj = jax.random.normal(ks[2], (C, H * D), dtype=jnp.float32) * 0.02
        bproj = jnp.zeros((C,), dtype=jnp.float32)
        temperature = jnp.ones((1, H, 1, 1), dtype=jnp.float32)
        return {'x': x, 'Wqkv': Wqkv, 'bqkv': bqkv, 'Wproj': Wproj, 'bproj': bproj, 'temperature': temperature}
    _L0_attn_all = _L0_attn_setup()
    _L0_attn_in = {k: v for k, v in _L0_attn_all.items() if k in ('Wqkv', 'bqkv', 'Wproj', 'bproj', 'temperature')}
    del _L0_attn_all

    def _L0_ffn_setup():
        import jax, jax.numpy as jnp
        import numpy as np
        D_MODEL = 64
        N_EXPERTS = 16
        HIDDEN = 128
        SCALE = 0.02
        key = jax.random.key(seed)
        ks = jax.random.split(key, 5)
        x = jax.random.normal(ks[0], (4, 2048, D_MODEL), dtype=jnp.float32)
        gate_w = jax.random.normal(ks[1], (D_MODEL, N_EXPERTS), dtype=jnp.float32) * SCALE
        gate_b = jnp.zeros((N_EXPERTS,), dtype=jnp.float32)
        w1 = jax.random.normal(ks[2], (N_EXPERTS, D_MODEL, HIDDEN), dtype=jnp.float32) * SCALE
        w2 = jax.random.normal(ks[3], (N_EXPERTS, D_MODEL, HIDDEN), dtype=jnp.float32) * SCALE
        w3 = jax.random.normal(ks[4], (N_EXPERTS, HIDDEN, D_MODEL), dtype=jnp.float32) * SCALE
        return {'x': x, 'gate_w': gate_w, 'gate_b': gate_b, 'w1': w1, 'w2': w2, 'w3': w3}
    _L0_ffn_all = _L0_ffn_setup()
    _L0_ffn_in = {k: v for k, v in _L0_ffn_all.items() if k in ('gate_w', 'gate_b', 'w1', 'w2', 'w3')}
    del _L0_ffn_all
    return {'x': x, 'L0_tok_A_log': _L0_tok_in['A_log'], 'L0_tok_D': _L0_tok_in['D'], 'L0_tok_W_dbc': _L0_tok_in['W_dbc'], 'L0_tok_W_dt': _L0_tok_in['W_dt'], 'L0_tok_b_dt': _L0_tok_in['b_dt'], 'L0_attn_Wqkv': _L0_attn_in['Wqkv'], 'L0_attn_bqkv': _L0_attn_in['bqkv'], 'L0_attn_Wproj': _L0_attn_in['Wproj'], 'L0_attn_bproj': _L0_attn_in['bproj'], 'L0_attn_temperature': _L0_attn_in['temperature'], 'L0_ffn_gate_w': _L0_ffn_in['gate_w'], 'L0_ffn_gate_b': _L0_ffn_in['gate_b'], 'L0_ffn_w1': _L0_ffn_in['w1'], 'L0_ffn_w2': _L0_ffn_in['w2'], 'L0_ffn_w3': _L0_ffn_in['w3']}

def reference(x, L0_tok_A_log, L0_tok_D, L0_tok_W_dbc, L0_tok_W_dt, L0_tok_b_dt, L0_attn_Wqkv, L0_attn_bqkv, L0_attn_Wproj, L0_attn_bproj, L0_attn_temperature, L0_ffn_gate_w, L0_ffn_gate_b, L0_ffn_w1, L0_ffn_w2, L0_ffn_w3):
    import jax
    import jax.numpy as jnp

    def _L0_tok_ref(x, A_log, D, W_dbc, W_dt, b_dt):
        import jax, jax.numpy as jnp
        import numpy as np
        BATCH = 2
        SEQ = 1024
        D_MODEL = 64
        N_STATE = 64
        DT_RANK = 1
        NUM_LAYERS = 3

        def _ssm_layer(x, A_log, Dp, W_dbc, W_dt, b_dt):
            A = -jnp.exp(A_log)
            dbc = jnp.einsum('ble,ce->blc', x, W_dbc)
            delta, Bm, Cm = jnp.split(dbc, [DT_RANK, DT_RANK + N_STATE], axis=-1)
            delta = jax.nn.softplus(jnp.einsum('blr,er->ble', delta, W_dt) + b_dt)
            dA = jnp.exp(delta[..., None] * A)
            dBx = (delta * x)[..., None] * Bm[:, :, None, :]

            def combine(c1, c2):
                a1, h1 = c1
                a2, h2 = c2
                return (a1 * a2, h1 * a2 + h2)
            _, hs = jax.lax.associative_scan(combine, (dA, dBx), axis=1)
            y = jnp.einsum('blen,bln->ble', hs, Cm)
            return y + Dp * x
        for i in range(NUM_LAYERS):
            x = _ssm_layer(x, A_log[i], D[i], W_dbc[i], W_dt[i], b_dt[i])
            if i < NUM_LAYERS - 1:
                b, l, d = x.shape
                x = x[:, :l // 2 * 2].reshape(b, l // 2, 2, d).mean(axis=2)
        return x

    def _L0_attn_ref(x, Wqkv, bqkv, Wproj, bproj, temperature):
        import jax, jax.numpy as jnp
        import numpy as np
        A, Bc, Cc = (0.5, 1.0, 1.0)
        H = 8
        EPS = 1e-12

        def _normalize(t):
            n = jnp.linalg.norm(t, axis=-1, keepdims=True)
            return t / jnp.maximum(n, EPS)
        B, N, C = x.shape
        D = C // H
        scale = float(D) ** 0.25
        qkv = (x @ Wqkv.T + bqkv).reshape(B, N, 3, H, D)
        qkv = jnp.transpose(qkv, (2, 0, 3, 1, 4))
        q, k, v = (qkv[0], qkv[1], qkv[2])
        q = q * scale
        v1 = jnp.concatenate([jnp.ones((B, H, N, 1), dtype=v.dtype), v], axis=-1)
        qn = _normalize(q) * (scale * temperature)
        kn = _normalize(k) * scale
        vN = v1 / N
        kv_mod = jnp.einsum('bhni,bhnj,bhne->bhije', kn, kn, vN)
        kv = jnp.einsum('bhnd,bhne->bhde', kn, vN)
        vsum = jnp.sum(vN, axis=-2)[:, :, None, :]
        y = A * jnp.einsum('bhni,bhnj,bhije->bhne', qn, qn, kv_mod) + scale ** 2 * Bc * jnp.einsum('bhnd,bhde->bhne', qn, kv) + scale ** 4 * Cc * vsum
        y_norm, y = (y[..., :1], y[..., 1:])
        y = y / y_norm
        out = jnp.transpose(y, (0, 2, 1, 3)).reshape(B, N, H * D)
        return out @ Wproj.T + bproj

    def _L0_ffn_ref(x, gate_w, gate_b, w1, w2, w3):
        import jax, jax.numpy as jnp
        import numpy as np
        D_MODEL = 64
        N_EXPERTS = 16
        HIDDEN = 128
        SCALE = 0.02
        n_experts = w1.shape[0]
        logits = jnp.einsum('bsd,de->bse', x, gate_w) + gate_b
        probs = jax.nn.softmax(logits, axis=-1)
        top_probs, top_idx = jax.lax.top_k(probs, 2)
        top_probs = top_probs / jnp.sum(top_probs, axis=-1, keepdims=True)
        dispatch = jnp.sum(jax.nn.one_hot(top_idx, n_experts, dtype=x.dtype) * top_probs[..., None], axis=-2)
        h1 = jnp.einsum('bsd,edh->bseh', x, w1)
        h2 = jnp.einsum('bsd,edh->bseh', x, w2)
        hidden = jax.nn.silu(h1) * h2
        expert_out = jnp.einsum('bseh,eho->bseo', hidden, w3)
        return jnp.einsum('bseo,bse->bso', expert_out, dispatch)
    h = _L0_tok_ref(x, L0_tok_A_log, L0_tok_D, L0_tok_W_dbc, L0_tok_W_dt, L0_tok_b_dt)
    h = h + _L0_attn_ref(_layernorm(h, axis=-1), L0_attn_Wqkv, L0_attn_bqkv, L0_attn_Wproj, L0_attn_bproj, L0_attn_temperature)
    h = h + _L0_ffn_ref(_layernorm(h, axis=-1), L0_ffn_gate_w, L0_ffn_gate_b, L0_ffn_w1, L0_ffn_w2, L0_ffn_w3)
    return h

_drawn_inputs = setup_inputs


def setup_inputs(seed=0):
    import zlib

    import numpy as np

    out = dict(_drawn_inputs(seed))
    spreads = {'L0_tok_D': (1.0, 0.2),
     'L0_tok_b_dt': (0.0, 0.734),
     'L0_attn_bqkv': (0.0, 0.346),
     'L0_attn_bproj': (0.0, 0.1),
     'L0_attn_temperature': (1.0, 0.6),
     'L0_ffn_gate_b': (0.0, 0.8)}
    factors = {'L0_tok_A_log': 6.278,
     'L0_tok_W_dt': 8.0,
     'L0_attn_Wqkv': 8.0,
     'L0_ffn_gate_w': 8.0,
     'L0_ffn_w1': 8.0,
     'L0_ffn_w2': 8.0,
     'L0_ffn_w3': 8.0}
    for name, (base, spread) in spreads.items():
        noise = np.random.default_rng([zlib.crc32(name.encode()), seed]).standard_normal(out[name].shape)
        drawn = base * np.exp(spread * noise) if base else spread * noise
        out[name] = jnp.asarray(drawn.astype(out[name].dtype))
    for name, factor in factors.items():
        out[name] = (out[name] * factor).astype(out[name].dtype)
    return out
```

```python
from contextlib import ExitStack

import concourse.bass as bass
from concourse import mybir

ALU = mybir.AluOpType
ACT = mybir.ActivationFunctionType
AXX = mybir.AxisListType.X
F32 = mybir.dt.float32
F32R = mybir.dt.float32r
BF16 = mybir.dt.bfloat16
I32 = mybir.dt.int32

BATCH, SEQ, C = 32, 750, 64
GROUPS, NB = 2, 8
NS = 64
LAYERS = 3
LEN = [750, 375, 187]
CW = [375, 375, 374]
NC = [16, 8, 4]
PEEL = 4
EXP_ZERO = -104.0
LN_EPS = 1e-5
H, D = 8, 8
NT = 187
TP = 94
TOK = 2 * TP
TILES = 2 * NB
UNITS = 2 * TILES
QKVW = 216
SETUP_V = 2
NE, TOPK, HID = 16, 2, 128
QUAD = 288
FT = 96
NORM_EPS = 1e-12
BIG_NEG = -3.0e38


def program(nc, a, out):
    SCALE = float(D) ** 0.25
    with ExitStack() as ctx:
        def sb(name, shape, dt=F32):
            return ctx.enter_context(nc.sbuf_tensor(name, shape, dt))

        def sem(name):
            return ctx.enter_context(nc.semaphore(name))

        pairs = [ctx.enter_context(nc.psum_tensor(f"pair{i}", [128, 2, 512], F32)) for i in range(4)]
        bank = [pairs[i // 2][:, i % 2, :] for i in range(8)]

        x0 = sb("x0", [128, NB * 750])
        big = sb("big", [128, 24000])
        Bn, Cn = big[:, 0:6000], big[:, 6000:12000]
        delta, u = big[:, 12000:18000], big[:, 18000:24000]
        xl = [x0[:, :], big[:, 3000:6000], big[:, 9000:9000 + NB * 187]]
        tmp = sb("tmp", [128, 3256])
        resid = sb("resid", [128, NB * TOK])

        ident = sb("ident", [128, 128])
        identb = sb("identb", [128, 128], BF16)
        blocks = sb("blocks", [128, 128])
        tri = sb("tri", [128, 128])
        slotno = sb("slotno", [128, NS])
        ridx = sb("ridx", [128, NE])
        featw = sb("featw", [FT, 4, 72])
        dsel = sb("dsel", [96, 2 * NE], BF16)
        wB = sb("wB", [128, LAYERS, 128])
        wC = sb("wC", [128, LAYERS, 128])
        wZ = sb("wZ", [128, LAYERS, 128])
        w0 = sb("w0", [128, LAYERS])
        wdt = sb("wdt", [128, LAYERS, 64])
        dskip = sb("dskip", [128, LAYERS])
        bdt = sb("bdt", [128, LAYERS])
        A = sb("A", [128, LAYERS, NS])
        AT = sb("AT", [64, LAYERS, 128])
        wqkv = sb("wqkv", [128, 384])
        bqkv = sb("bqkv", [128, 384])
        wproj = sb("wproj", [128, 128])
        bproj = sb("bproj", [128, 1])
        nscale = sb("nscale", [128, 16])
        fscale = sb("fscale", [128, 16])
        gatew = sb("gatew", [128, NE])
        gateb = sb("gateb", [128, NE])
        w1h = sb("w1h", [128, NE * HID], F32R)
        w1l = sb("w1l", [128, NE * HID], F32R)
        w2h = sb("w2h", [128, NE * HID], F32R)
        w2l = sb("w2l", [128, NE * HID], F32R)
        w3 = sb("w3", [128, NE, 64])
        xs = sb("xs", [128, 2, NB * TOK], F32R)
        d3T = sb("d3T", [96, NB * TOK], BF16)
        ones64 = sb("ones64", [64, 1])

        mins = sb("mins", [128, 16])
        minall = sb("minall", [128, 1])
        amax2 = sb("amax2", [128, 2, NS])
        amx = sb("amx", [128, 1])
        fast = sb("fast", [128, 1])
        slow = sb("slow", [128, 1])
        rank = sb("rank", [128, 1])
        fastblk = sb("fastblk", [128, 128])
        onehot = sb("onehot", [128, NS])
        count = sb("count", [1, 1], I32)
        Aslot = sb("Aslot", [128, NS])

        def two(at, n):
            return [tmp[:, at + n * j:at + n * j + n] for j in range(2)]

        eT, rT, uT, lT = (two(750 * k, 375) for k in range(4))
        bcT, gT = eT, rT
        dA, hT = two(0, 750), two(1500, 750)
        sel = tmp[:, 3000:3128]

        tokT = big[0:TP, 0:2048]
        xc = big[0:TP, 2048:4096]
        xT = big[:, 4096:4096 + TILES * TP]
        attT = [big[:, 5000 + TOK * j:5000 + TOK * j + TOK] for j in range(2)]
        qkv = big[0:TP, 5600:5600 + UNITS * QKVW].rearrange("p (u w) -> p u w", w=QKVW)
        sq = big[0:TP, 12512:12512 + 4096]
        kF = big[0:TP, 16608:16608 + 16 * QUAD].rearrange("p (u f) -> p u f", f=QUAD)
        qF = big[0:TP, 0:16 * QUAD].rearrange("p (u f) -> p u f", f=QUAD)
        kvm = [big[0:FT, 21216 + 576 * j:21792 + 576 * j].rearrange("p (b f) -> p b f", b=2) for j in range(2)]
        qT = [big[0:FT, 22368 + 376 * j:22744 + 376 * j] for j in range(2)]
        att = [big[0:TP, 23120 + 256 * j:23376 + 256 * j] for j in range(2)]
        norm = big[0:TP, 21216:21728]
        xhl = big[0:TP, 4096:8192].rearrange("p (u k c) -> p u k c", k=2, c=64)
        lg, eq, mask, rest, mask2 = (big[0:TP, 16608 + 512 * k:17120 + 512 * k].rearrange(
            "p (u e) -> p u e", e=NE) for k in range(5))
        d3 = sb("d3", [TP, UNITS, 48], BF16)
        small = sb("small", [TP, 8, UNITS])
        sT, tT = two(0, 376), two(752, 376)
        hidT = [tmp[:, 1504 + 376 * j:1880 + 376 * j] for j in range(4)]

        S = LAYERS
        waited = sem("waited")
        params_in = sem("params_in")
        later_in = sem("later_in")
        staged = sem("staged")
        split_v = sem("split_v")
        zeroed = sem("zeroed")
        setup_v = sem("setup_v")
        setup_a = sem("setup_a")
        x_in = sem("x_in")
        proj = [sem(f"proj{i}") for i in range(S)]
        evac = [sem(f"evac{i}") for i in range(S)]
        absd = [sem(f"absd{i}") for i in range(S)]
        relud = [sem(f"relud{i}") for i in range(S)]
        expd = [sem(f"expd{i}") for i in range(S)]
        onep = [sem(f"onep{i}") for i in range(S)]
        lnd = [sem(f"lnd{i}") for i in range(S)]
        wsum = [sem(f"wsum{i}") for i in range(S)]
        corr = [sem(f"corr{i}") for i in range(S)]
        dlt = [sem(f"dlt{i}") for i in range(S)]
        udone = [sem(f"udone{i}") for i in range(S)]
        dec_v = [sem(f"dec_v{i}") for i in range(S)]
        dec_p = [sem(f"dec_p{i}") for i in range(S)]
        bcd = [sem(f"bcd{i}") for i in range(S)]
        gsum = [sem(f"gsum{i}") for i in range(S)]
        ug = [sem(f"ug{i}") for i in range(S)]
        y0 = [sem(f"y0{i}") for i in range(S)]
        seld = [sem(f"seld{i}") for i in range(S)]
        bcast = [sem(f"bcast{i}") for i in range(S)]
        decay = [sem(f"decay{i}") for i in range(S)]
        scan = [sem(f"scan{i}") for i in range(S)]
        hc = [sem(f"hc{i}") for i in range(S)]
        ysum = [sem(f"ysum{i}") for i in range(S)]
        pooled = sem("pooled")
        tok_p, tok_a = sem("tok_p"), sem("tok_a")
        ln_v, ln_a = sem("ln_v"), sem("ln_a")
        xt_p, xt_a = sem("xt_p"), sem("xt_a")
        qkv_p, qkv_v = sem("qkv_p"), sem("qkv_v")
        nrm_v, nrm_a = sem("nrm_v"), sem("nrm_a")
        qf_v, kf_g = sem("qf_v"), sem("kf_g")
        ones_g = sem("ones_g")
        kv_p, kv_v = sem("kv_p"), sem("kv_v")
        qt_p, qt_a = sem("qt_p"), sem("qt_a")
        yat_p, yat_v = sem("yat_p"), sem("yat_v")
        rec_v = sem("rec_v")
        at_p, at_a = sem("at_p"), sem("at_a")
        pr_p, pr_v = sem("pr_p"), sem("pr_v")
        gt_p, gt_v, gt_a = sem("gt_p"), sem("gt_v"), sem("gt_a")
        dt_p, dt_a = sem("dt_p"), sem("dt_a")
        h1_p, h2_p = sem("h1_p"), sem("h2_p")
        dw_p = sem("dw_p")
        silu_a = sem("silu_a")
        sd_v = sem("sd_v")
        hid_v = sem("hid_v")
        down_p = sem("down_p")
        out_v = sem("out_v")
        out_d = sem("out_d")

        first, later = [], []
        for k in range(2):
            blk = slice(64 * k, 64 * k + 64)
            for i in range(S):
                first += [(wB[blk, i, blk], a["w_tok"][:, i, 1:65]), (wC[blk, i, blk], a["w_tok"][:, i, 65:129])]
            first.append((w0[blk, :], a["w_tok0"]))
            later += [(wqkv[blk, 192 * k:192 * k + 192], a["wqkv"]), (wproj[blk, blk], a["wproj"]),
                      (gatew[blk, :], a["gate_w"])]
        dsel32 = tmp[0:96, 0:2 * NE]
        first += [(wdt[:, :, :], a["wdt"]), (bdt[:, :], a["bdt"]), (dskip[:, :], a["dskip"]), (A[:, :, :], a["alog"]),
                  (AT[:, :, :], a["alogT"]), (dsel32, a["dsel"])]
        first += [(t[:, :], a[n]) for t, n in (
            (ident, "ident"), (blocks, "blocks"), (tri, "tri"), (slotno, "slotno"))]
        first.append((fscale[:, 0:8], a["temp"]))
        later += [(t[:, :], a[n]) for t, n in (
            (bqkv, "bqkv"), (bproj, "bproj"), (gateb, "gate_b"), (nscale, "nscale"), (ridx, "ridx"))]
        later += [(featw[:, :, :], a["featw"]), (w3[:, :, :], a["w3"])]
        PARAMS, LATER = 16 * len(first), 16 * len(later)

        KU = [n // 2 for n in NC]
        STEP = [3, 3, 5]
        TOKN, LNN, LNA, XTN = 8, 16, 4, 12
        DECV, DECP, GTN = 10, 3, 23
        FF = NE * 2
        FCH = NB // 2

        def col(t, c, w):
            return t[:, bass.ds(c * w, w)]

        def wait_alone(eng, sem, value):
            eng.wait_ge(sem, value)
            eng.sem_inc(waited, 1)

        def over_slots(eng, skip, work):
            n = eng.value_load(count[0:1, 0:1], min_val=0, max_val=NS)
            with eng.Fori(0, PEEL) as s:
                with eng.If(n > s):
                    work(s)
                with eng.Else():
                    skip(s, 1)
            with eng.If(n > PEEL):
                with eng.Fori(PEEL, NS) as s:
                    work(s)
            with eng.Else():
                skip(PEEL, NS - PEEL)
            eng.nop()

        block = ctx.enter_context(nc.Block())

        @block.sync
        def _(sp):
            sp.sem_inc(out_d, 16)
            sp.dma_start(x0[:, :], a["x"][:, 0, :]).then_inc(x_in, 16)
            sp.wait_ge(zeroed, 2)
            for dst, src in later:
                sp.dma_start(dst, src).then_inc(later_in, 16)
            with sp.Fori(0, GROUPS) as g:
                with sp.If(g < 1):
                    sp.wait_ge(pooled, g * 3 + 1)
                    for i, name in enumerate(("w1", "w2")):
                        for k in range(2):
                            sp.dma_start(x0[64 * k:64 * k + 64, 2048 * i:2048 * i + 2048], a[name]).then_inc(staged, 16)
                    sp.wait_ge(split_v, 2)
                with sp.Else():
                    sp.nop()
                with sp.If(g < GROUPS - 1):
                    sp.wait_ge(pooled, g * 3 + 1)
                    sp.dma_start(x0[:, :], a["x"][:, 1, :]).then_inc(x_in, 16)
                with sp.Else():
                    sp.nop()
                with sp.Fori(0, FCH) as j:
                    sp.wait_ge(out_v, g * FCH + j + 2)
                    sp.dma_start(out[:, bass.ds((g * FCH + j) * 2, 2), :],
                                 resid[:, bass.ds(j * 2 * TOK, 2 * TOK)].rearrange("p (b t) -> p b t", b=2)[:, :, 0:NT]
                                 ).then_inc(out_d, 16)
            sp.wait_ge(out_d, 16 * (FCH * GROUPS + 1))

        @block.tensor
        def _(pe):
            for i in range(S):
                pe.sem_inc(gsum[i], 2)
                pe.sem_inc(bcast[i], KU[i])
            pe.sem_inc(yat_p, 8)
            pe.sem_inc(at_p, 2)
            pe.sem_inc(pr_p, 2)
            pe.sem_inc(down_p, 4)

            def scan_layer(g, l):
                n, w, U, x = NC[l], CW[l], KU[l], xl[l]
                if l:
                    wait_alone(pe, pooled, g * 3 + l)
                else:
                    wait_alone(pe, x_in, g * 16 + 16)
                with pe.Fori(0, n // 2) as i:
                    for k in range(2):
                        c = i * 2 + k
                        pe.wait_ge(evac[l], g * n + c + 1)
                        pe.wait_ge(relud[l], g * n + c + 1)
                        pe.matmul(bank[k][:, 0:w], wB[:, l, :], col(x, c, w), start=True, stop=True)
                        pe.matmul(bank[2 + k][:, 0:w], wC[:, l, :], col(x, c, w), start=True, stop=True)
                        pe.matmul(bank[4 + k][:, 0:w], wZ[:, l, :], col(x, c, w), start=True, stop=True)\
                            .then_inc(proj[l], 1)
                pe.wait_ge(dec_v[l], g * DECV + 2)
                pe.transpose(bank[6][:, 0:128], amax2[:, :, :].rearrange("p a n -> p (a n)"), ident[:, :])\
                    .then_inc(dec_p[l], 1)
                pe.wait_ge(dec_v[l], g * DECV + 5)
                pe.matmul(bank[6][:, 128:129], tri[:, :], slow[:, :], start=True, stop=True)
                pe.matmul(bank[6][0:1, 130:131], slow[0:64, :], ones64[:, :], start=True, stop=True)\
                    .then_inc(dec_p[l], 1)
                pe.wait_ge(dec_v[l], g * DECV + 9)
                pe.matmul(bank[6][:, 256:256 + NS], AT[:, l, :], onehot[0:64, :], start=True, stop=True)\
                    .then_inc(dec_p[l], 1)
                wait_alone(pe, dec_v[l], g * DECV + 10)
                with pe.Fori(0, n // 2) as i:
                    for k in range(2):
                        c = i * 2 + k
                        pe.wait_ge(bcd[l], g * n + c + 1)
                        pe.wait_ge(ug[l], g * n + c + 1)
                        pe.matmul(bank[6 + k][:, 0:w], fastblk[:, :], bcT[k][:, 0:w], start=True, stop=True)\
                            .then_inc(gsum[l], 1)
                wait_alone(pe, ug[l], g * n + n + 2)

                def work(s):
                    wait_alone(pe, seld[l], (g * NS + s) + 2)
                    with pe.Fori(0, U // 2) as i:
                        for k in range(2):
                            q = i * 2 + k
                            pe.wait_ge(hc[l], (g * NS + s) * U + q + 1)
                            for b in range(2):
                                pe.matmul(pairs[k][:, b, 0:w], sel, col(Bn, q * 2 + b, w), start=True, stop=True)
                            for b in range(2):
                                mm = pe.matmul(pairs[2 + k][:, b, 0:w], sel, col(Cn, q * 2 + b, w), start=True, stop=True)
                            mm.then_inc(bcast[l], 1)

                def skip(s, m):
                    pe.wait_ge(bcast[l], (g * NS + s) * U + U)
                    pe.sem_inc(bcast[l], m * U)

                over_slots(pe, skip, work)

            def tokens_out(g, r):
                for j in range(4):
                    for t in range(4):
                        mm = pe.transpose(bank[j][0:TP, 128 * t:128 * t + 128],
                                          resid[:, (4 * j + t) * TP:(4 * j + t + 1) * TP], ident[:, :])
                    mm.then_inc(tok_p, 1)

            def attention(g):
                pe.wait_ge(later_in, LATER)
                pe.wait_ge(pooled, g * 3 + 3)
                tokens_out(g, 0)
                pe.wait_ge(ln_v, g * LNN + 7)
                for j in range(4):
                    for t in range(4):
                        i = 4 * j + t
                        mm = pe.transpose(bank[4 + j][:, TP * t:TP * t + TP], xc[:, 128 * i:128 * i + 128],
                                          ident[0:TP, 0:TP])
                    mm.then_inc(xt_p, 1)
                for i in range(TILES):
                    if i % 4 == 0:
                        pe.wait_ge(xt_a, g * XTN + i // 4 + 1)
                    pe.wait_ge(qkv_v, g * TILES + i + 1)
                    pe.matmul(bank[i % 4][0:TP, 0:384], xT[:, TP * i:TP * i + TP], wqkv[:, :], start=True, stop=True)\
                        .then_inc(qkv_p, 1)

                def q_features(t):
                    pe.wait_ge(qt_a, g * UNITS + t + 1)
                    b = bank[4 + t % 2]
                    for f in range(3):
                        pe.transpose(b[0:FT, TP * f:TP * f + TP], qF[:, t % 16, FT * f:FT * f + FT], ident[0:TP, 0:TP])
                    pe.transpose(b[0:FT, TP * 3:TP * 4], qkv[:, t, 0:FT], ident[0:TP, 0:TP]).then_inc(qt_p, 1)

                def attend(t, n):
                    pe.wait_ge(qt_a, g * UNITS + t + 3)
                    for f in range(4):
                        mm = pe.matmul(bank[6 + n % 2][0:TP, 72 * (t % 4):72 * (t % 4) + 72],
                                       qT[t % 2][:, TP * f:TP * f + TP], kvm[n % 2][:, t % 2, 72 * f:72 * f + 72],
                                       start=(f == 0), stop=(f == 3))
                    mm.then_inc(yat_p, 1)

                def att_transpose(n):
                    pe.wait_ge(yat_v, g * NB + n + 3)
                    for p in range(2):
                        mm = pe.transpose(bank[6 + n % 2][:, 288 + TP * p:288 + TP * p + TP],
                                          att[n % 2][:, 128 * p:128 * p + 128], ident[0:TP, 0:TP])
                    mm.then_inc(at_p, 1)

                def project(n):
                    pe.wait_ge(at_a, g * NB + n + 1)
                    pe.matmul(pairs[n % 2][:, 1, 288:288 + TOK], wproj[:, :], attT[n % 2], start=True, stop=True)\
                        .then_inc(pr_p, 1)

                pe.wait_ge(nrm_v, g * 7 + 7)
                pe.wait_ge(ones_g, g * 2 + 2)
                for n in range(NB):
                    if n % 4 == 0:
                        pe.wait_ge(kf_g, g * 2 + n // 4 + 1)
                        pe.wait_ge(qf_v, g * 2 + n // 4 + 1)
                    pe.wait_ge(kv_v, g * NB + n + 1)
                    pe.wait_ge(pr_v, g * NB + n + 1)
                    for b in range(2):
                        for f in range(4):
                            for p in range(2):
                                unit = (2 * n + p) * 2 + b
                                rows = TP - p
                                feat = kF[0:rows, unit % 16, FT * f:FT * f + FT] if f < 3 else qkv[0:rows, unit, 72:72 + FT]
                                mm = pe.matmul(pairs[n % 2][0:FT, b, 72 * f:72 * f + 72], feat, qkv[0:rows, unit, 136:208],
                                               start=(p == 0), stop=(p == 1))
                    mm.then_inc(kv_p, 1)
                    q_features(4 * n)
                    q_features(4 * n + 1)
                    if n:
                        att_transpose(n - 1)
                    pe.wait_ge(kv_v, g * NB + n + 3)
                    pe.wait_ge(yat_v, g * NB + n + 1)
                    pe.wait_ge(at_a, g * NB + n - 1) if n > 1 else None
                    attend(4 * n, n)
                    q_features(4 * n + 2)
                    if n:
                        project(n - 1)
                    attend(4 * n + 1, n)
                    q_features(4 * n + 3)
                    attend(4 * n + 2, n)
                    attend(4 * n + 3, n)
                att_transpose(NB - 1)
                project(NB - 1)
                pe.wait_ge(pr_v, g * NB + NB + 2)
                tokens_out(g, 1)
                pe.wait_ge(ln_v, g * LNN + LNN)
                pe.wait_ge(tok_a, g * TOKN + 8)
                for b in range(2):
                    for j in range(4):
                        for t in range(4):
                            i = 4 * j + t
                            mm = pe.transpose(bank[4 * b + j][:, TP * t:TP * t + TP],
                                              xhl[:, 2 * i + b, :, :].rearrange("p k c -> p (k c)"), ident[0:TP, 0:TP])
                        mm.then_inc(xt_p, 1)
                pe.wait_ge(xt_a, g * XTN + 12)
                for t in range(UNITS):
                    mm = pe.matmul(bank[0][0:TP, NE * t:NE * t + NE],
                                   xs[:, t % 2, TP * (t // 2):TP * (t // 2) + TP].bitcast(F32), gatew[:, :],
                                   start=True, stop=True)
                mm.then_inc(gt_p, 1)
                pe.wait_ge(gt_v, g * GTN + GTN)
                for j in range(2):
                    b16 = bank[2 + j].bitcast(BF16)
                    for t in range(8):
                        i = 8 * j + t
                        mm = pe.transpose(b16[0:96, TP * t:TP * t + TP],
                                          d3[:, 2 * i:2 * i + 2, :].rearrange("p b e -> p (b e)"), identb[0:TP, 0:TP])
                    mm.then_inc(dt_p, 1)

            def experts(g):
                pe.wait_ge(split_v, 2)
                wait_alone(pe, dt_a, g * 2 + 2)
                with pe.Fori(0, FCH) as j:
                    step0 = (g * FCH + j) * FF

                    xj = [xs[:, b, bass.ds(j * 2 * TOK, 2 * TOK)] for b in range(2)]
                    dj = d3T[:, bass.ds(j * 2 * TOK, 2 * TOK)]

                    def up(e, b, hi, lo, dst, signal):
                        cols = slice(HID * e, HID * e + HID)
                        pe.matmul(dst, hi[:, cols], xj[b], start=True, stop=False)
                        pe.matmul(dst, lo[:, cols], xj[b], start=False, stop=True).then_inc(signal, 1)

                    def down(e):
                        for b in range(2):
                            i = 2 * e + b
                            pe.wait_ge(hid_v, step0 + i + 3)
                            pe.matmul(bank[6][64 * b:64 * b + 64, 0:2 * TOK], w3[:, e, :], hidT[i % 4],
                                      start=(e == 0), stop=(e == NE - 1)).then_inc(down_p, 1)

                    for e in range(NE):
                        for b in range(2):
                            pe.wait_ge(silu_a, step0 + 2 * e + b + 1)
                            up(e, b, w1h, w1l, bank[b][:, 0:2 * TOK], h1_p)
                        for b in range(2):
                            pe.wait_ge(sd_v, step0 + 2 * e + b + 1)
                            c = NE * b + e
                            pe.matmul(bank[4 + b][:, 0:2 * TOK], dsel[:, c:c + 1].to_broadcast([96, 128]), dj,
                                      start=True, stop=True).then_inc(dw_p, 1)
                        for b in range(2):
                            pe.wait_ge(hid_v, step0 + 2 * e + b + 1)
                            up(e, b, w2h, w2l, bank[2 + b][:, 0:2 * TOK], h2_p)
                        if e == 1:
                            pe.wait_ge(out_v, g * FCH + j + 1)
                        if e:
                            down(e - 1)
                    down(NE - 1)

            pe.wait_ge(params_in, PARAMS)
            pe.wait_ge(setup_v, SETUP_V)
            with pe.Fori(0, GROUPS) as g:
                pe.wait_ge(out_v, g * FCH + 1)
                for l in range(S):
                    scan_layer(g, l)
                attention(g)
                experts(g)

        @block.scalar
        def _(act):
            for i in range(S):
                act.sem_inc(evac[i], 2)
                act.sem_inc(seld[i], 1)
                act.sem_inc(decay[i], 2)
            act.sem_inc(qt_a, 2)
            act.sem_inc(silu_a, 2)

            def scan_layer(g, l):
                n, w, U = NC[l], CW[l], KU[l]
                act.preload_act_table_set("natural_log_exp_and_others")
                with act.Fori(0, n // 2) as i:
                    for k in range(2):
                        c = i * 2 + k
                        act.wait_ge(proj[l], g * n + c + 1)
                        act.wait_ge(dlt[l], g * n + c + 1)
                        act.activation(eT[k][:, 0:w], bank[4 + k][:, 0:w], ACT.Abs, bias=bdt[:, l:l + 1])\
                            .then_inc(absd[l], 1)
                        act.activation(col(Bn, c, w), bank[k][:, 0:w], ACT.Copy)
                        act.activation(col(Cn, c, w), bank[2 + k][:, 0:w], ACT.Copy).then_inc(evac[l], 1)
                        act.wait_ge(absd[l], g * n + c + 1)
                        act.activation(eT[k][:, 0:w], eT[k][:, 0:w], ACT.Exp, scale=-1.0).then_inc(expd[l], 1)
                        act.wait_ge(expd[l], g * n + c + 1)
                        act.activation(lT[k][:, 0:w], eT[k][:, 0:w], ACT.Ln, bias=1.0).then_inc(lnd[l], 1)
                act.wait_ge(dec_v[l], g * DECV + 10)
                wait_alone(act, y0[l], g * n + n)

                def work(s):
                    wait_alone(act, bcast[l], (g * NS + s) * U + U)
                    act.activation(sel, blocks[:, :], ACT.Copy, scale=onehot[:, bass.ds(s, 1)]).then_inc(seld[l], 1)
                    with act.Fori(0, U // 2) as i:
                        for k in range(2):
                            q = i * 2 + k
                            wait_alone(act, scan[l], ((g * NS + s) * U + q + 1) * STEP[l])
                            act.activation(dA[k][:, 0:2 * w], col(delta, q, 2 * w), ACT.Exp,
                                           scale=Aslot[:, bass.ds(s, 1)]).then_inc(decay[l], 1)

                def skip(s, m):
                    act.wait_ge(decay[l], (g * NS + s) * U + 2)
                    act.sem_inc(seld[l], m)
                    act.sem_inc(decay[l], m * U)

                over_slots(act, skip, work)

            def copy_out(sem_in, at, dst, src, sem_out):
                act.wait_ge(sem_in, at)
                act.activation(dst, src, ACT.Copy).then_inc(sem_out, 1)

            def layer_norm(g, r):
                for j in range(4):
                    copy_out(tok_p, g * TOKN + 4 * r + j + 1, tokT[:, 512 * j:512 * j + 512], bank[j][0:TP, :], tok_a)
                act.wait_ge(ln_v, g * LNN + 7 * r + 3)
                act.activation(sq[:, 0:2048], xc, ACT.Square).then_inc(ln_a, 1)
                act.wait_ge(ln_v, g * LNN + 7 * r + 5)
                act.activation(small[:, 1, :], small[:, 1, :], ACT.Sqrt).then_inc(ln_a, 1)

            def attention(g):
                layer_norm(g, 0)
                for j in range(4):
                    copy_out(xt_p, g * XTN + j + 1, xT[:, 4 * TP * j:4 * TP * j + 4 * TP], bank[4 + j][:, 0:4 * TP], xt_a)
                act.wait_ge(qkv_v, g * TILES + TILES + 4)
                act.activation(sq.rearrange("p (u k c) -> p u k c", k=2, c=64),
                               qkv[:, :, 0:144].rearrange("p u (k c) -> p u k c", k=2)[:, :, :, 0:64], ACT.Square)\
                    .then_inc(nrm_a, 1)
                act.wait_ge(nrm_v, g * 7 + 1)
                act.activation(norm, norm, ACT.Sqrt).then_inc(nrm_a, 1)
                for n in range(NB):
                    for t in range(4 * n, 4 * n + 4):
                        act.wait_ge(yat_p, g * UNITS + t + 7)
                        copy_out(qt_p, g * UNITS + t + 1, qT[t % 2], bank[4 + t % 2][0:FT, 0:4 * TP], qt_a)
                        if n and t % 4 == 1:
                            attention_transposed(g, n - 1)
                attention_transposed(g, NB - 1)
                layer_norm(g, 1)
                for t in range(8):
                    b, j = divmod(t, 4)
                    copy_out(xt_p, g * XTN + 4 + t + 1, xs[:, b, 4 * TP * j:4 * TP * j + 4 * TP], bank[t][:, 0:4 * TP], xt_a)
                act.wait_ge(gt_v, g * GTN + 14)
                act.activation(lg, lg, ACT.Exp).then_inc(gt_a, 1)
                for j in range(2):
                    copy_out(dt_p, g * 2 + j + 1, d3T[:, 8 * TP * j:8 * TP * j + 8 * TP],
                             bank[2 + j].bitcast(BF16)[0:96, 0:8 * TP], dt_a)

            def attention_transposed(g, n):
                act.wait_ge(pr_p, g * NB + n + 1)
                copy_out(at_p, g * NB + n + 3, attT[n % 2], bank[6 + n % 2][:, 288:288 + TOK], at_a)

            def experts(g):
                act.preload_act_table(ACT.Silu)
                with act.Fori(0, FCH) as j:
                    step0 = (g * FCH + j) * FF
                    for i in range(FF):
                        act.wait_ge(h1_p, step0 + i + 1)
                        act.wait_ge(sd_v, step0 + i + 1)
                        act.activation(sT[i % 2], bank[i % 2][:, 0:2 * TOK], ACT.Silu).then_inc(silu_a, 1)

            act.wait_ge(zeroed, 1)
            for dst, src in first:
                act.dma_start(dst, src).then_inc(params_in, 16)
            act.wait_ge(params_in, PARAMS)
            act.wait_ge(setup_v, 1)
            act.activation(A[:, :, :], A[:, :, :], ACT.Exp).then_inc(setup_a, 1)
            act.activation(AT[:, :, :], AT[:, :, :], ACT.Exp).then_inc(setup_a, 1)
            with act.Fori(0, GROUPS) as g:
                for l in range(S):
                    scan_layer(g, l)
                attention(g)
                experts(g)

        @block.vector
        def _(v):
            for i in range(S):
                v.sem_inc(dlt[i], 2)
                v.sem_inc(relud[i], 2)
                v.sem_inc(ug[i], 2)
                v.sem_inc(scan[i], 2 * STEP[i])
                v.sem_inc(hc[i], 2)
            v.sem_inc(qkv_v, 4)
            v.sem_inc(kv_v, 2)
            v.sem_inc(yat_v, 2)
            v.sem_inc(pr_v, 2)
            v.sem_inc(sd_v, 2)
            v.sem_inc(hid_v, 2)
            v.sem_inc(out_v, 1)

            def setup():
                v.memset(wB[:, :, :], 0.0)
                v.memset(wC[:, :, :], 0.0).then_inc(zeroed, 1)
                v.memset(wqkv[:, :], 0.0)
                v.memset(wproj[:, :], 0.0).then_inc(zeroed, 1)
                v.memset(wZ[:, :, :], 0.0)
                v.memset(resid[:, :], 0.0)
                v.memset(ones64[:, :], 1.0)
                v.memset(fscale[:, 8:16], SCALE).then_inc(zeroed, 1)
                v.wait_ge(zeroed, 3)
                v.wait_ge(params_in, PARAMS)
                v.tensor_scalar(A[:, :, :], A[:, :, :], 88.0, None, ALU.min)
                v.tensor_scalar(AT[:, :, :], AT[:, :, :], 88.0, None, ALU.min).then_inc(setup_v, 1)
                v.tensor_scalar(wC[:, 0:2, :], wC[:, 0:2, :], 0.5, None, ALU.mult)
                v.tensor_scalar(dskip[:, 0:2], dskip[:, 0:2], 0.5, None, ALU.mult)
                v.tensor_scalar(fscale[:, 0:8], fscale[:, 0:8], SCALE * SCALE, None, ALU.mult)
                v.tensor_copy(identb[:, :], ident[:, :])
                v.tensor_copy(dsel[:, :], dsel32)
                for l in range(S):
                    for k in range(2):
                        blk = slice(64 * k, 64 * k + 64)
                        v.tensor_scalar(wZ[blk, l, blk], wdt[blk, l, :], w0[blk, l:l + 1], None, ALU.mult)
                v.wait_ge(setup_a, 2)
                v.tensor_scalar(A[:, :, :], A[:, :, :], -1.0, None, ALU.mult)
                v.tensor_scalar(AT[:, :, :], AT[:, :, :], -1.0, None, ALU.mult).then_inc(setup_v, 1)

            def split_experts():
                v.wait_ge(staged, 64)
                v.tensor_copy(w1h[:, :], x0[:, 0:2048])
                v.tensor_copy(w2h[:, :], x0[:, 2048:4096]).then_inc(split_v, 1)
                v.wait_ge(split_v, 1)
                v.tensor_tensor(w1l[:, :], x0[:, 0:2048], w1h[:, :].bitcast(F32), ALU.subtract)
                v.tensor_tensor(w2l[:, :], x0[:, 2048:4096], w2h[:, :].bitcast(F32), ALU.subtract).then_inc(split_v, 1)

            def scan_layer(g, l):
                n, w, U, x = NC[l], CW[l], KU[l], xl[l]
                with v.Fori(0, n // 2) as i:
                    for k in range(2):
                        c = i * 2 + k
                        v.wait_ge(absd[l], g * n + c + 1)
                        v.tensor_scalar(rT[k][:, 0:w], bank[4 + k][:, 0:w], bdt[:, l:l + 1], 0.0, ALU.add, ALU.max)\
                            .then_inc(relud[l], 1)
                        v.wait_ge(onep[l], g * n + c + 1)
                        e, t = eT[k][:, 0:w], uT[k][:, 0:w]
                        v.scalar_tensor_tensor(t, t, 1.0, e, ALU.subtract, ALU.subtract, reverse1=True)\
                            .then_inc(corr[l], 1)
                        v.wait_ge(corr[l], g * n + c + 1)
                        v.wait_ge(wsum[l], g * n + c + 1)
                        v.tensor_tensor(col(delta, c, w), t, lT[k][:, 0:w], ALU.add).then_inc(dlt[l], 1)
                        v.wait_ge(dlt[l], g * n + c + 3)
                        v.tensor_reduce(mins[:, bass.ds(c, 1)], col(delta, c, w), AXX, ALU.min)
                        v.tensor_tensor(col(u, c, w), col(delta, c, w), col(x, c, w), ALU.mult).then_inc(udone[l], 1)

                step = [0]

                def then(ins, last=True):
                    if last:
                        step[0] += 1
                        ins.then_inc(dec_v[l], 1)
                        v.wait_ge(dec_v[l], g * DECV + step[0])

                v.wait_ge(udone[l], g * n + n)
                then(v.tensor_reduce(minall[:, :], mins[:, 0:n], AXX, ALU.min))
                v.tensor_scalar(amax2[:, 0, :], A[:, l, :], minall[:, :], None, ALU.mult)
                then(v.tensor_scalar(amax2[:, 1, :], A[:, l, :], minall[:, :], None, ALU.mult))
                v.wait_ge(dec_p[l], g * DECP + 1)
                then(v.tensor_reduce(amx[:, :], bank[6][:, 0:128], AXX, ALU.max))
                then(v.tensor_scalar(fast[:, :], amx[:, :], EXP_ZERO, None, ALU.is_le))
                then(v.tensor_scalar(slow[:, :], fast[:, :], -1.0, 1.0, ALU.mult, ALU.add))
                then(v.tensor_scalar(fastblk[:, :], blocks[:, :], fast[:, :], None, ALU.mult))
                v.wait_ge(dec_p[l], g * DECP + 2)
                then(v.tensor_copy(rank[:, :], bank[6][:, 128:129]))
                then(v.tensor_copy(count[:, :], bank[6][0:1, 130:131]))
                then(v.tensor_scalar(onehot[:, :], slotno[:, :], rank[:, :], slow[:, :], ALU.is_equal, ALU.mult))
                v.wait_ge(dec_p[l], g * DECP + 3)
                v.tensor_copy(Aslot[:, :], bank[6][:, 256:256 + NS]).then_inc(dec_v[l], 1)
                assert step[0] == DECV - 1

                with v.Fori(0, n // 2) as i:
                    for k in range(2):
                        c = i * 2 + k
                        v.wait_ge(gsum[l], g * n + c + 3)
                        v.tensor_tensor(gT[k][:, 0:w], bank[6 + k][:, 0:w], col(u, c, w), ALU.mult).then_inc(ug[l], 1)
                        v.wait_ge(ug[l], g * n + c + 3)
                        v.scalar_tensor_tensor(col(x, c, w), col(x, c, w), dskip[:, l:l + 1], gT[k][:, 0:w],
                                               ALU.mult, ALU.add).then_inc(y0[l], 1)

                def work(s):
                    with v.Fori(0, U // 2) as i:
                        for k in range(2):
                            q = i * 2 + k
                            unit = (g * NS + s) * U + q
                            h = hT[k]
                            v.wait_ge(bcast[l], unit + 1 + U)
                            bu = pairs[k][:, :, 0:w]
                            v.tensor_tensor(bu, bu, col(u, q, 2 * w).rearrange("p (b t) -> p b t", b=2), ALU.mult)\
                                .then_inc(scan[l], 1)
                            v.wait_ge(decay[l], unit + 3)
                            v.wait_ge(ysum[l], unit + 1)
                            parts = STEP[l] - 1
                            m = 2 * w // parts
                            for p in range(parts):
                                v.wait_ge(scan[l], (unit + 2) * STEP[l] + (1 + p if l == 0 else 1))
                                b, off = divmod(p * m, w)
                                first = h[:, p * m - 1:p * m] if l == 0 and p else 0.0
                                v.tensor_tensor_scan(h[:, p * m:p * m + m], dA[k][:, p * m:p * m + m],
                                                     pairs[k][:, b, off:off + m], first, ALU.mult, ALU.add)\
                                    .then_inc(scan[l], 1)
                            v.wait_ge(scan[l], (unit + 3) * STEP[l])
                            h2 = h[:, 0:2 * w].rearrange("p (b t) -> p b t", b=2)
                            v.tensor_tensor(h2, h2, pairs[2 + k][:, :, 0:w], ALU.mult).then_inc(hc[l], 1)

                def skip(s, m):
                    v.wait_ge(hc[l], (g * NS + s) * U + 2)
                    v.sem_inc(scan[l], m * U * STEP[l])
                    v.sem_inc(hc[l], m * U)

                over_slots(v, skip, work)
                v.wait_ge(ysum[l], (g + 1) * NS * U + 2)
                v.wait_ge(y0[l], g * n + n)
                if l < S - 1:
                    L2 = LEN[l + 1]
                    y = x.rearrange("p (b t) -> p b t", b=NB)[:, :, 0:2 * L2].rearrange("p b (t k) -> p b t k", k=2)
                    v.tensor_tensor(xl[l + 1].rearrange("p (b t) -> p b t", b=NB), y[:, :, :, 0], y[:, :, :, 1], ALU.add)\
                        .then_inc(pooled, 1)
                else:
                    v.wait_ge(out_d, g * FCH * 16 + 16)
                    v.tensor_copy(resid[:, :].rearrange("p (b t) -> p b t", b=NB)[:, :, 0:NT],
                                  x.rearrange("p (b t) -> p b t", b=NB)).then_inc(pooled, 1)

            def bc(t, m):
                return t.unsqueeze(len(t.shape)).to_broadcast(list(t.shape) + [m])

            def over(t, m, at):
                shape = list(t.shape)
                shape.insert(at, m)
                return t.unsqueeze(at).to_broadcast(shape)

            def layer_norm(g, r):
                step = [7 * r]

                def then(ins):
                    step[0] += 1
                    ins.then_inc(ln_v, 1)
                    v.wait_ge(ln_v, g * LNN + step[0])

                tok3, xc3 = (t.rearrange("p (u c) -> p u c", c=64) for t in (tokT, xc))
                v.wait_ge(tok_a, g * TOKN + 4 * r + 4)
                then(v.tensor_reduce(small[:, 0, :], tok3, AXX, ALU.add))
                then(v.tensor_scalar(small[:, 0, :], small[:, 0, :], 1.0 / 64, None, ALU.mult))
                then(v.tensor_tensor(xc3, tok3, bc(small[:, 0, :], 64), ALU.subtract))
                v.wait_ge(ln_a, g * LNA + 2 * r + 1)
                then(v.tensor_reduce(small[:, 1, :], sq[:, 0:2048].rearrange("p (u c) -> p u c", c=64), AXX, ALU.add))
                then(v.tensor_scalar(small[:, 1, :], small[:, 1, :], 1.0 / 64, LN_EPS, ALU.mult, ALU.add))
                v.wait_ge(ln_a, g * LNA + 2 * r + 2)
                then(v.reciprocal(small[:, 1, :], small[:, 1, :]))
                then(v.tensor_tensor(xc3, xc3, bc(small[:, 1, :], 64), ALU.mult))
                if r:
                    hi = xhl[:, :, 0, :]
                    then(v.tensor_copy(hi.bitcast(F32R), xc3))
                    then(v.tensor_tensor(xhl[:, :, 1, :], xc3, hi, ALU.subtract))

            def attention(g):
                v.wait_ge(later_in, LATER)
                layer_norm(g, 0)
                for i in range(TILES):
                    v.wait_ge(qkv_p, g * TILES + i + 1)
                    dst = qkv[:, 2 * i:2 * i + 2, :].rearrange("p b (k c) -> p b k c", c=72)[:, :, :, 0:64]
                    v.tensor_tensor(dst, bank[i % 4][0:TP, 0:384].rearrange("p (b k c) -> p b k c", b=2, k=3),
                                    bqkv[0:TP, :].rearrange("p (b k c) -> p b k c", b=2, k=3), ALU.add).then_inc(qkv_v, 1)
                step = [0]

                def then(ins, done=True):
                    if done:
                        step[0] += 1
                        ins.then_inc(nrm_v, 1)
                        v.wait_ge(nrm_v, g * 7 + step[0])

                v.wait_ge(nrm_a, g * 2 + 1)
                then(v.tensor_reduce(norm, sq.rearrange("p (n d) -> p n d", d=D), AXX, ALU.add))
                norm3 = norm.rearrange("p (u h) -> p u h", h=16)
                v.wait_ge(nrm_a, g * 2 + 2)
                then(v.tensor_tensor(norm3, norm3, over(nscale[0:TP, :], UNITS, 1), ALU.mult))
                then(v.tensor_scalar(norm, norm, NORM_EPS, None, ALU.max))
                then(v.reciprocal(norm, norm))
                then(v.tensor_tensor(norm3, norm3, over(fscale[0:TP, :], UNITS, 1), ALU.mult))
                q4 = qkv[:, :, 0:64].rearrange("p u (h d) -> p u h d", d=D)
                k4 = qkv[:, :, 72:136].rearrange("p u (h d) -> p u h d", d=D)
                then(v.tensor_tensor(q4, q4, bc(norm3[:, :, 0:8], D), ALU.mult))
                then(v.tensor_tensor(k4, k4, bc(norm3[:, :, 8:16], D), ALU.mult))

                def residual(n):
                    v.wait_ge(pr_p, g * NB + n + 3)
                    r = resid[:, TOK * n:TOK * n + TOK]
                    v.scalar_tensor_tensor(r, pairs[n % 2][:, 1, 288:288 + TOK], bproj[:, :], r, ALU.add, ALU.add)\
                        .then_inc(pr_v, 1)

                for n in range(NB):
                    if n % 4 == 0:
                        v.wait_ge(qt_p, g * UNITS + 4 * n) if n else None
                        part = q4[:, 4 * n:4 * n + 16, :, :]
                        products(v, qF, part).then_inc(qf_v, 1)
                    v.wait_ge(kv_p, g * NB + n + 1)
                    v.wait_ge(yat_p, g * UNITS + 4 * n + 4)
                    v.tensor_tensor(kvm[n % 2], pairs[n % 2][0:FT, :, 0:288],
                                    over(featw[:, :, :].rearrange("p f c -> p (f c)"), 2, 1), ALU.mult).then_inc(kv_v, 1)
                    if n:
                        residual(n - 1)
                    v.wait_ge(yat_p, g * UNITS + 4 * n + 12)
                    v.wait_ge(at_p, g * NB + n + 1)
                    y = bank[6 + n % 2][0:TP, 0:288].rearrange("p (u c) -> p u c", c=72)
                    rec = small[:, 2, :]
                    v.reciprocal(rec.rearrange("p (u h) -> p u h", h=8), y[:, :, 0:8]).then_inc(rec_v, 1)
                    v.wait_ge(rec_v, g * NB + n + 1)
                    v.tensor_tensor(att[n % 2].rearrange("p (u h d) -> p u h d", u=4, d=D),
                                    y[:, :, 8:72].rearrange("p u (h d) -> p u h d", d=D),
                                    bc(rec.rearrange("p (u h) -> p u h", h=8), D), ALU.mult).then_inc(yat_v, 1)
                residual(NB - 1)
                layer_norm(g, 1)
                gating(g)

            def gating(g):
                step = [0]

                def then(ins):
                    step[0] += 1
                    ins.then_inc(gt_v, 1)
                    v.wait_ge(gt_v, g * GTN + step[0])

                m1, first, m2, den = (small[:, 3 + k, :] for k in range(4))
                v.wait_ge(gt_p, g + 1)
                then(v.tensor_tensor(lg, bank[0][0:TP, :].rearrange("p (u e) -> p u e", e=NE),
                                     over(gateb[0:TP, :], UNITS, 1), ALU.add))
                then(v.tensor_reduce(m1, lg, AXX, ALU.max))

                def first_of(src, top, dst):
                    then(v.tensor_tensor(eq, src, bc(top, NE), ALU.is_equal))
                    then(v.tensor_tensor(eq, eq, over(ridx[0:TP, :], UNITS, 1), ALU.mult))
                    then(v.tensor_reduce(first, eq, AXX, ALU.max))
                    then(v.tensor_tensor(dst, eq, bc(first, NE), ALU.is_equal))

                first_of(lg, m1, mask)
                then(v.scalar_tensor_tensor(rest, mask, BIG_NEG, lg, ALU.mult, ALU.add))
                then(v.tensor_reduce(m2, rest, AXX, ALU.max))
                first_of(rest, m2, mask2)
                then(v.tensor_tensor(mask, mask, mask2, ALU.add))
                then(v.tensor_tensor(lg, lg, bc(m1, NE), ALU.subtract))
                v.wait_ge(gt_a, g + 1)
                then(v.tensor_tensor(lg, lg, mask, ALU.mult))
                then(v.tensor_reduce(den, lg, AXX, ALU.add))
                then(v.reciprocal(den, den))
                then(v.tensor_tensor(lg, lg, bc(den, NE), ALU.mult))
                then(v.tensor_copy(d3[:, :, 0:16], lg))
                then(v.tensor_tensor(lg, lg, d3[:, :, 0:16], ALU.subtract))
                then(v.tensor_copy(d3[:, :, 16:32], lg))
                then(v.tensor_tensor(lg, lg, d3[:, :, 16:32], ALU.subtract))
                v.tensor_copy(d3[:, :, 32:48], lg).then_inc(gt_v, 1)
                assert step[0] == GTN - 1

            def experts(g):
                with v.Fori(0, FCH) as j:
                    step0 = (g * FCH + j) * FF
                    for i in range(FF):
                        k = i % 2
                        v.wait_ge(silu_a, step0 + i + 3)
                        v.wait_ge(dw_p, step0 + i + 1)
                        v.tensor_tensor(tT[k], bank[4 + k][:, 0:2 * TOK], sT[k], ALU.mult).then_inc(sd_v, 1)
                        v.wait_ge(sd_v, step0 + i + 3)
                        v.wait_ge(h2_p, step0 + i + 1)
                        v.wait_ge(down_p, step0 + i + 1)
                        v.tensor_tensor(hidT[i % 4], bank[2 + k][:, 0:2 * TOK], tT[k], ALU.mult).then_inc(hid_v, 1)
                    v.wait_ge(down_p, step0 + FF + 4)
                    r = resid[:, bass.ds(j * 2 * TOK, 2 * TOK)]
                    v.tensor_tensor(r, bank[6][:, 0:2 * TOK], r, ALU.add).then_inc(out_v, 1)

            setup()
            with v.Fori(0, GROUPS) as g:
                for l in range(S):
                    scan_layer(g, l)
                    if l == 1:
                        with v.If(g < 1):
                            split_experts()
                        with v.Else():
                            v.nop()
                attention(g)
                experts(g)

        @block.gpsimd
        def _(pool):
            for i in range(S):
                pool.sem_inc(ysum[i], 2)

            def scan_layer(g, l):
                n, w, U, x = NC[l], CW[l], KU[l], xl[l]
                with pool.Fori(0, n // 2) as i:
                    for k in range(2):
                        c = i * 2 + k
                        wait_alone(pool, expd[l], g * n + c + 1)
                        pool.tensor_scalar(uT[k][:, 0:w], eT[k][:, 0:w], 1.0, 1.0, ALU.mult, ALU.add).then_inc(onep[l], 1)
                        pool.wait_ge(relud[l], g * n + c + 3)
                        pool.wait_ge(lnd[l], g * n + c + 1)
                        pool.tensor_tensor(lT[k][:, 0:w], lT[k][:, 0:w], rT[k][:, 0:w], ALU.add).then_inc(wsum[l], 1)
                wait_alone(pool, dlt[l], g * n + n + 2)
                with pool.Fori(0, n // 2) as i:
                    for k in range(2):
                        c = i * 2 + k
                        pool.wait_ge(gsum[l], g * n + c + 1)
                        pool.tensor_tensor(bcT[k][:, 0:w], col(Bn, c, w), col(Cn, c, w), ALU.mult).then_inc(bcd[l], 1)
                wait_alone(pool, dec_v[l], g * DECV + 10)

                def work(s):
                    with pool.Fori(0, U // 2) as i:
                        for k in range(2):
                            q = i * 2 + k
                            unit = (g * NS + s) * U + q
                            pool.wait_ge(hc[l], unit + 3)
                            pool.wait_ge(ysum[l], unit + 2)
                            y = col(x, q, 2 * w)
                            pool.tensor_tensor(y, y, hT[k][:, 0:2 * w], ALU.add).then_inc(ysum[l], 1)

                def skip(s, m):
                    pool.wait_ge(ysum[l], (g * NS + s) * U + 2)
                    pool.sem_inc(ysum[l], m * U)

                over_slots(pool, skip, work)

            def attention(g):
                wait_alone(pool, pooled, g * 3 + 3)
                pool.memset(qkv[:, :, 64:72], 1.0).then_inc(ones_g, 1)
                pool.memset(qkv[:, :, 136:144], 1.0).then_inc(ones_g, 1)
                k4 = qkv[:, :, 72:136].rearrange("p u (h d) -> p u h d", d=D)
                pool.wait_ge(nrm_v, g * 7 + 7)
                for n in range(0, NB, 4):
                    if n:
                        pool.wait_ge(kv_p, g * NB + n)
                    products(pool, kF, k4[:, 4 * n:4 * n + 16, :, :]).then_inc(kf_g, 1)

            with pool.Fori(0, GROUPS) as g:
                for l in range(S):
                    scan_layer(g, l)
                attention(g)


def products(eng, dst, t):
    at = 0
    for k in range(D):
        m = D - k
        ins = eng.tensor_tensor(dst[:, :, at:at + H * m].rearrange("p u (h d) -> p u h d", d=m),
                                t[:, :, :, 0:m], t[:, :, :, k:D], ALU.mult)
        at += H * m
    return ins



def shape_constants():
    import numpy as np
    f = np.float32
    half = np.arange(128) // 64
    featw = np.zeros((FT * 4, 72), f)
    scale2 = D ** 0.5

    def put(row, head, weight):
        featw[row, head] = weight
        featw[row, 8 + 8 * head:16 + 8 * head] = weight

    row = 0
    for k in range(D):
        for head in range(H):
            for _ in range(D - k):
                put(row, head, 0.5 if k == 0 else 1.0)
                row += 1
    for i in range(64):
        put(QUAD + i, i // D, scale2)
    for head in range(H):
        put(QUAD + 64 + head, head, scale2 * scale2)
    dsel = np.zeros((2, 3, NE, 2 * NE), f)
    for b in range(2):
        for e in range(NE):
            dsel[b, :, e, NE * b + e] = 1
    n = np.arange(64)
    tri = np.zeros((128, 128), f)
    tri[:64] = np.tile((n[:, None] < n[None, :]).astype(f), (1, 2))
    return {
        "ident": np.eye(128, dtype=f), "blocks": (half[:, None] == half[None, :]).astype(f), "tri": tri,
        "slotno": np.tile(np.arange(NS, dtype=f), (128, 1)), "ridx": np.tile(np.arange(NE, 0, -1, dtype=f), (128, 1)),
        "featw": np.ascontiguousarray(featw.reshape(4, FT, 72).transpose(1, 0, 2)),
        "dsel": dsel.reshape(6 * NE, 2 * NE),
        "nscale": np.tile(np.array([float(D) ** 0.25] * 8 + [1.0] * 8, f), (128, 1)),
    }


def laid_out(i):
    import numpy as np
    i = {k: np.asarray(x) for k, x in i.items()}

    def rows(x, n=128):
        return np.tile(x.reshape(1, -1), (n, 1))

    x = i["x"].reshape(2, 16, SEQ, C).transpose(0, 3, 1, 2)
    w = i["L0_tok_W_dbc"].transpose(2, 0, 1)
    alog = i["L0_tok_A_log"]
    a = {
        "x": x.reshape(128, GROUPS, NB * SEQ),
        "w_tok": w, "w_tok0": w[:, :, 0],
        "wdt": rows(i["L0_tok_W_dt"]).reshape(128, LAYERS, 64),
        "alog": np.tile(alog.transpose(1, 0, 2), (2, 1, 1)),
        "alogT": np.tile(alog.transpose(2, 0, 1), (1, 1, 2)),
        "dskip": np.tile(i["L0_tok_D"].T, (2, 1)), "bdt": np.tile(i["L0_tok_b_dt"].T, (2, 1)),
        "wqkv": i["L0_attn_Wqkv"].T, "bqkv": rows(np.tile(i["L0_attn_bqkv"], 2)),
        "wproj": i["L0_attn_Wproj"].T, "bproj": np.tile(i["L0_attn_bproj"][:, None], (2, 1)),
        "temp": rows(i["L0_attn_temperature"]), "gate_w": i["L0_ffn_gate_w"], "gate_b": rows(i["L0_ffn_gate_b"]),
        "w1": i["L0_ffn_w1"].transpose(1, 0, 2).reshape(64, NE * HID),
        "w2": i["L0_ffn_w2"].transpose(1, 0, 2).reshape(64, NE * HID),
        "w3": i["L0_ffn_w3"].transpose(1, 0, 2),
    }
    return {k: np.ascontiguousarray(x) for k, x in (a | shape_constants()).items()}


def kernel(**inputs):
    import numpy as np
    import concourse.bacc as bacc
    from concourse.bass_utils import run_bass_kernel_spmd

    nc = bacc.Bacc("TRN2", target_bir_lowering=False, num_devices=1)
    arrays = {f"in_{k}": x for k, x in laid_out(inputs).items()}
    a = {k[3:]: nc.dram_tensor(k, x.shape, mybir.dt.from_np(x.dtype), kind="ExternalInput").ap()
         for k, x in arrays.items()}
    out = nc.dram_tensor("out", (128, 16, NT), F32, kind="ExternalOutput").ap()
    program(nc, a, out)
    r = run_bass_kernel_spmd(nc, [arrays], core_ids=[0])
    y = np.asarray(r.results[0]["out"]).reshape(2, C, 16, NT)
    return np.ascontiguousarray(y.transpose(0, 2, 3, 1)).reshape(BATCH, NT, C)
```

```python
from contextlib import ExitStack

import concourse.bass as bass
from concourse import mybir

ALU = mybir.AluOpType
ACT = mybir.ActivationFunctionType
AXX = mybir.AxisListType.X
F32 = mybir.dt.float32
F32R = mybir.dt.float32r
BF16 = mybir.dt.bfloat16
I32 = mybir.dt.int32

BATCH, SEQ, C = 32, 750, 64
GROUPS, NB = 2, 8
NS = 64
LAYERS = 3
LEN = [750, 375, 187]
CW = [375, 375, 374]
NC = [16, 8, 4]
PEEL = 4
EXP_ZERO = -104.0
LN_EPS = 1e-5
H, D = 8, 8
NT = 187
TP = 94
TOK = 2 * TP
TILES = 2 * NB
QUARTERS = NB // 2
QC = 2 * TOK
QU = 8
QKVW = 216
SETUP_V = 2
NE, TOPK, HID = 16, 2, 128
QUAD = 288
FEATS = QUAD + 72
FT, FTN = 120, 3
NORM_EPS = 1e-12
BIG_NEG = -3.0e38


def program(nc, a, out):
    SCALE = float(D) ** 0.25
    with ExitStack() as ctx:
        def sb(name, shape, dt=F32):
            return ctx.enter_context(nc.sbuf_tensor(name, shape, dt))

        def sem(name):
            return ctx.enter_context(nc.semaphore(name))

        pairs = [ctx.enter_context(nc.psum_tensor(f"pair{i}", [128, 2, 512], F32)) for i in range(4)]
        bank = [pairs[i // 2][:, i % 2, :] for i in range(8)]

        x0 = sb("x0", [128, NB * 750])
        big = sb("big", [128, 24000])
        Bn, Cn = big[:, 0:6000], big[:, 6000:12000]
        delta, u = big[:, 12000:18000], big[:, 18000:24000]
        xl = [x0[:, :], big[:, 3000:6000], big[:, 9000:9000 + NB * 187]]
        tmp = sb("tmp", [128, 3256])
        resid = sb("resid", [128, NB * TOK])

        ident = sb("ident", [128, 128])
        identb = sb("identb", [128, 128], BF16)
        blocks = sb("blocks", [128, 128])
        tri = sb("tri", [128, 128])
        slotno = sb("slotno", [128, NS])
        ridx = sb("ridx", [128, NE])
        featw = sb("featw", [FT, 2 * FTN, 64])
        dsel = sb("dsel", [96, 2 * NE], BF16)
        wB = sb("wB", [128, LAYERS, 128])
        wC = sb("wC", [128, LAYERS, 128])
        wZ = sb("wZ", [128, LAYERS, 128])
        w0 = sb("w0", [128, LAYERS])
        wdt = sb("wdt", [128, LAYERS, 64])
        dskip = sb("dskip", [128, LAYERS])
        bdt = sb("bdt", [128, LAYERS])
        A = sb("A", [128, LAYERS, NS])
        AT = sb("AT", [64, LAYERS, 128])
        wqkv = sb("wqkv", [128, 384])
        bqkv = sb("bqkv", [128, 384])
        wproj = sb("wproj", [128, 128])
        bproj = sb("bproj", [128, 1])
        centering = sb("centering", [128, 128])
        averaging = sb("averaging", [128, 128])
        eps = sb("eps", [128, 1])
        floor = sb("floor", [128, 16])
        fscale = sb("fscale", [128, 16])
        gatew = sb("gatew", [128, 2 * NE])
        gateb = sb("gateb", [128, NE])
        w1h = sb("w1h", [128, NE * HID], F32R)
        w1l = sb("w1l", [128, NE * HID], F32R)
        w2h = sb("w2h", [128, NE * HID], F32R)
        w2l = sb("w2l", [128, NE * HID], F32R)
        w3 = sb("w3", [128, NE, 64])
        xs = sb("xs", [128, 2, NB * TOK], F32R)
        d3T = sb("d3T", [96, NB * TOK], BF16)
        ones64 = sb("ones64", [64, 1])

        mins = sb("mins", [128, 16])
        minall = sb("minall", [128, 1])
        amax2 = sb("amax2", [128, 2, NS])
        amx = sb("amx", [128, 1])
        fast = sb("fast", [128, 1])
        slow = sb("slow", [128, 1])
        rank = sb("rank", [128, 1])
        fastblk = sb("fastblk", [128, 128])
        onehot = sb("onehot", [128, NS])
        count = sb("count", [1, 1], I32)
        Aslot = sb("Aslot", [128, NS])

        def two(at, n):
            return [tmp[:, at + n * j:at + n * j + n] for j in range(2)]

        eT, rT, uT, lT = (two(750 * k, 375) for k in range(4))
        bcT, gT = eT, rT
        dA, hT = two(0, 750), two(1500, 750)
        sel = tmp[:, 3000:3128]

        def pick(at, rows, n, count=2):
            return [big[0:rows, at + n * j:at + n * j + n] for j in range(count)]

        qF, kF = (([t.rearrange("p (u f) -> p u f", f=FEATS) for t in pick(at, TP, QU * FEATS)])
                  for at in (0, 12672))
        qkv = big[0:TP, 5760:5760 + 4 * QU * QKVW].rearrange("p (u w) -> p u w", w=QKVW)
        kvm = [t.rearrange("p (k f c) -> p k f c", k=2, c=64)
               for t in pick(18432, FT, 4 * FTN * 64)]
        qT = [t.rearrange("p (f c) -> p f c", c=QC) for t in pick(19968, FT, FTN * QC)]
        attT = pick(22224, 128, QC)
        norm = [t.rearrange("p (u h) -> p u h", h=16) for t in pick(22976, TP, QU * 16, QUARTERS)]
        sqT, xn = two(0, QC), two(2 * QC, QC)
        sq = tmp[0:TP, 4 * QC:4 * QC + QU * 128]
        lg, eq, mask, rest, mask2 = (tmp[0:TP, 2528 + 128 * k:2656 + 128 * k].rearrange(
            "p (u e) -> p u e", e=NE) for k in range(5))
        small = big[0:TP, 23488:23520].rearrange("p (k u) -> p k u", u=QU)
        d3 = sb("d3", [TP, 2, QU, 48], BF16)
        sT, tT = two(0, 376), two(752, 376)
        hidT = [tmp[:, 1504 + 376 * j:1880 + 376 * j] for j in range(4)]

        S = LAYERS
        waited = sem("waited")
        params_in = sem("params_in")
        later_in = sem("later_in")
        staged = sem("staged")
        split_v = sem("split_v")
        zeroed = sem("zeroed")
        setup_v = sem("setup_v")
        setup_a = sem("setup_a")
        x_in = sem("x_in")
        proj = [sem(f"proj{i}") for i in range(S)]
        evac = [sem(f"evac{i}") for i in range(S)]
        absd = [sem(f"absd{i}") for i in range(S)]
        relud = [sem(f"relud{i}") for i in range(S)]
        expd = [sem(f"expd{i}") for i in range(S)]
        onep = [sem(f"onep{i}") for i in range(S)]
        lnd = [sem(f"lnd{i}") for i in range(S)]
        wsum = [sem(f"wsum{i}") for i in range(S)]
        corr = [sem(f"corr{i}") for i in range(S)]
        dlt = [sem(f"dlt{i}") for i in range(S)]
        udone = [sem(f"udone{i}") for i in range(S)]
        dec_v = [sem(f"dec_v{i}") for i in range(S)]
        dec_p = [sem(f"dec_p{i}") for i in range(S)]
        bcd = [sem(f"bcd{i}") for i in range(S)]
        gsum = [sem(f"gsum{i}") for i in range(S)]
        ug = [sem(f"ug{i}") for i in range(S)]
        y0 = [sem(f"y0{i}") for i in range(S)]
        seld = [sem(f"seld{i}") for i in range(S)]
        bcast = [sem(f"bcast{i}") for i in range(S)]
        decay = [sem(f"decay{i}") for i in range(S)]
        scan = [sem(f"scan{i}") for i in range(S)]
        hc = [sem(f"hc{i}") for i in range(S)]
        ysum = [sem(f"ysum{i}") for i in range(S)]
        pooled = sem("pooled")
        cen_p, var_p = sem("cen_p"), sem("var_p")
        csq_a, dev_a = sem("csq_a"), sem("dev_a")
        xn_v = sem("xn_v")
        qkv_p, qkv_v = sem("qkv_p"), sem("qkv_v")
        nrm_v, nrm_a = sem("nrm_v"), sem("nrm_a")
        qf_v, kf_g = sem("qf_v"), sem("kf_g")
        lin_a = sem("lin_a")
        ones_g = sem("ones_g")
        kv_p, kv_v = sem("kv_p"), sem("kv_v")
        qt_p, qt_a = sem("qt_p"), sem("qt_a")
        at_p = sem("at_p")
        rec_a = sem("rec_a")
        att_v = sem("att_v")
        pr_p, pr_v = sem("pr_p"), sem("pr_v")
        gt_p, gt_v, gt_a = sem("gt_p"), sem("gt_v"), sem("gt_a")
        dup_p = sem("dup_p")
        hi_a, lo_v = sem("hi_a"), sem("lo_v")
        dt_p, dt_a = sem("dt_p"), sem("dt_a")
        h1_p, h2_p = sem("h1_p"), sem("h2_p")
        dw_p = sem("dw_p")
        silu_a = sem("silu_a")
        sd_v = sem("sd_v")
        hid_v = sem("hid_v")
        down_p = sem("down_p")
        out_v = sem("out_v")
        out_d = sem("out_d")

        first, later = [], []
        for k in range(2):
            blk = slice(64 * k, 64 * k + 64)
            for i in range(S):
                first += [(wB[blk, i, blk], a["w_tok"][:, i, 1:65]), (wC[blk, i, blk], a["w_tok"][:, i, 65:129])]
            first.append((w0[blk, :], a["w_tok0"]))
            later += [(wqkv[blk, 192 * k:192 * k + 192], a["wqkv"]), (wproj[blk, blk], a["wproj"]),
                      (gatew[blk, NE * k:NE * k + NE], a["gate_w"])]
        dsel32 = tmp[0:96, 0:2 * NE]
        first += [(wdt[:, :, :], a["wdt"]), (bdt[:, :], a["bdt"]), (dskip[:, :], a["dskip"]), (A[:, :, :], a["alog"]),
                  (AT[:, :, :], a["alogT"]), (dsel32, a["dsel"])]
        first += [(t[:, :], a[n]) for t, n in (
            (ident, "ident"), (blocks, "blocks"), (tri, "tri"), (slotno, "slotno"))]
        first.append((fscale[:, 0:8], a["temp"]))
        later += [(t[:, :], a[n]) for t, n in (
            (bqkv, "bqkv"), (bproj, "bproj"), (gateb, "gate_b"), (floor, "floor"), (ridx, "ridx"),
            (centering, "centering"), (averaging, "averaging"))]
        later += [(featw[:, :, :], a["featw"]), (w3[:, :, :], a["w3"])]
        PARAMS, LATER = 16 * len(first), 16 * len(later)

        KU = [n // 2 for n in NC]
        STEP = [3, 3, 5]
        DECV, DECP = 10, 3
        Q, LN = QUARTERS, 2 * QUARTERS
        NRV, NRA, GTN = 5, 3, 23
        FF = NE * 2
        FCH = QUARTERS

        def col(t, c, w):
            return t[:, bass.ds(c * w, w)]

        def wait_alone(eng, sem, value):
            eng.wait_ge(sem, value)
            eng.sem_inc(waited, 1)

        def over_slots(eng, skip, work):
            n = eng.value_load(count[0:1, 0:1], min_val=0, max_val=NS)
            with eng.Fori(0, PEEL) as s:
                with eng.If(n > s):
                    work(s)
                with eng.Else():
                    skip(s, 1)
            with eng.If(n > PEEL):
                with eng.Fori(PEEL, NS) as s:
                    work(s)
            with eng.Else():
                skip(PEEL, NS - PEEL)
            eng.nop()

        block = ctx.enter_context(nc.Block())

        @block.sync
        def _(sp):
            sp.sem_inc(out_d, 16)
            sp.dma_start(x0[:, :], a["x"][:, 0, :]).then_inc(x_in, 16)
            sp.wait_ge(zeroed, 2)
            for dst, src in later:
                sp.dma_start(dst, src).then_inc(later_in, 16)
            with sp.Fori(0, GROUPS) as g:
                with sp.If(g < 1):
                    sp.wait_ge(pooled, g * 3 + 1)
                    for i, name in enumerate(("w1", "w2")):
                        for k in range(2):
                            sp.dma_start(x0[64 * k:64 * k + 64, 2048 * i:2048 * i + 2048], a[name]).then_inc(staged, 16)
                    sp.wait_ge(split_v, 2)
                with sp.Else():
                    sp.nop()
                with sp.If(g < GROUPS - 1):
                    sp.wait_ge(pooled, g * 3 + 1)
                    sp.dma_start(x0[:, :], a["x"][:, 1, :]).then_inc(x_in, 16)
                with sp.Else():
                    sp.nop()
                with sp.Fori(0, FCH) as j:
                    sp.wait_ge(out_v, g * FCH + j + 2)
                    sp.dma_start(out[:, bass.ds((g * FCH + j) * 2, 2), :],
                                 resid[:, bass.ds(j * 2 * TOK, 2 * TOK)].rearrange("p (b t) -> p b t", b=2)[:, :, 0:NT]
                                 ).then_inc(out_d, 16)
            sp.wait_ge(out_d, 16 * (FCH * GROUPS + 1))

        @block.tensor
        def _(pe):
            for i in range(S):
                pe.sem_inc(gsum[i], 2)
                pe.sem_inc(bcast[i], KU[i])
            pe.sem_inc(at_p, 2)
            pe.sem_inc(down_p, 4)

            def scan_layer(g, l):
                n, w, U, x = NC[l], CW[l], KU[l], xl[l]
                if l:
                    wait_alone(pe, pooled, g * 3 + l)
                else:
                    wait_alone(pe, x_in, g * 16 + 16)
                with pe.Fori(0, n // 2) as i:
                    for k in range(2):
                        c = i * 2 + k
                        pe.wait_ge(evac[l], g * n + c + 1)
                        pe.wait_ge(relud[l], g * n + c + 1)
                        pe.matmul(bank[k][:, 0:w], wB[:, l, :], col(x, c, w), start=True, stop=True)
                        pe.matmul(bank[2 + k][:, 0:w], wC[:, l, :], col(x, c, w), start=True, stop=True)
                        pe.matmul(bank[4 + k][:, 0:w], wZ[:, l, :], col(x, c, w), start=True, stop=True)\
                            .then_inc(proj[l], 1)
                pe.wait_ge(dec_v[l], g * DECV + 2)
                pe.transpose(bank[6][:, 0:128], amax2[:, :, :].rearrange("p a n -> p (a n)"), ident[:, :])\
                    .then_inc(dec_p[l], 1)
                pe.wait_ge(dec_v[l], g * DECV + 5)
                pe.matmul(bank[6][:, 128:129], tri[:, :], slow[:, :], start=True, stop=True)
                pe.matmul(bank[6][0:1, 130:131], slow[0:64, :], ones64[:, :], start=True, stop=True)\
                    .then_inc(dec_p[l], 1)
                pe.wait_ge(dec_v[l], g * DECV + 9)
                pe.matmul(bank[6][:, 256:256 + NS], AT[:, l, :], onehot[0:64, :], start=True, stop=True)\
                    .then_inc(dec_p[l], 1)
                wait_alone(pe, dec_v[l], g * DECV + 10)
                with pe.Fori(0, n // 2) as i:
                    for k in range(2):
                        c = i * 2 + k
                        pe.wait_ge(bcd[l], g * n + c + 1)
                        pe.wait_ge(ug[l], g * n + c + 1)
                        pe.matmul(bank[6 + k][:, 0:w], fastblk[:, :], bcT[k][:, 0:w], start=True, stop=True)\
                            .then_inc(gsum[l], 1)
                wait_alone(pe, ug[l], g * n + n + 2)

                def work(s):
                    wait_alone(pe, seld[l], (g * NS + s) + 2)
                    with pe.Fori(0, U // 2) as i:
                        for k in range(2):
                            q = i * 2 + k
                            pe.wait_ge(hc[l], (g * NS + s) * U + q + 1)
                            for b in range(2):
                                pe.matmul(pairs[k][:, b, 0:w], sel, col(Bn, q * 2 + b, w), start=True, stop=True)
                            for b in range(2):
                                mm = pe.matmul(pairs[2 + k][:, b, 0:w], sel, col(Cn, q * 2 + b, w), start=True, stop=True)
                            mm.then_inc(bcast[l], 1)

                def skip(s, m):
                    pe.wait_ge(bcast[l], (g * NS + s) * U + U)
                    pe.sem_inc(bcast[l], m * U)

                over_slots(pe, skip, work)

            def attention(g):
                def center(r, m, dst):
                    pe.matmul(dst[:, 0:QC], centering[:, :], resid[:, QC * r:QC * r + QC], start=True, stop=True)\
                        .then_inc(cen_p, 1)

                def variance(r, m, dst):
                    pe.wait_ge(csq_a, g * LN + m + 1)
                    pe.matmul(dst[:, 0:QC], averaging[:, :], sqT[r % 2], start=True, stop=True).then_inc(var_p, 1)

                def project_qkv(r):
                    pe.wait_ge(xn_v, g * LN + r + 1)
                    for i in range(4 * r, 4 * r + 4):
                        pe.wait_ge(qkv_v, g * TILES + i + 1)
                        pe.matmul(bank[i % 4][0:TP, 0:384], xn[r % 2][:, TP * (i % 4):TP * (i % 4) + TP], wqkv[:, :],
                                  start=True, stop=True).then_inc(qkv_p, 1)

                def moments(n):
                    r = n // 2
                    if n % 2 == 0:
                        pe.wait_ge(kf_g, g * Q + r + 1)
                        pe.wait_ge(lin_a, (g * Q + r) * 2 + 2)
                    pe.wait_ge(kv_v, g * NB + n + 1)
                    for b in range(2):
                        for f in range(FTN):
                            for p in range(2):
                                unit = (2 * n + p) * 2 + b
                                rows = TP - p
                                at = 65 * (FTN * b + f)
                                mm = pe.matmul(bank[n % 2][0:FT, at:at + 65],
                                               kF[r % 2][0:rows, unit % QU, FT * f:FT * f + FT],
                                               qkv[0:rows, unit, 143:208], start=(p == 0), stop=(p == 1))
                    mm.then_inc(kv_p, 1)

                def q_features(n):
                    r = n // 2
                    if n % 2 == 0:
                        pe.wait_ge(qf_v, g * Q + r + 1)
                    for f in range(FTN):
                        t = FTN * n + f
                        pe.wait_ge(qt_a, g * FTN * NB + t + 1)
                        for b in range(2):
                            for p in range(2):
                                at = TP * (2 * b + p)
                                mm = pe.transpose(bank[2 + t % 2][0:FT, at:at + TP],
                                                  qF[r % 2][:, ((2 * n + p) * 2 + b) % QU, FT * f:FT * f + FT],
                                                  ident[0:TP, 0:TP])
                        mm.then_inc(qt_p, 1)

                def attend(n):
                    pe.wait_ge(kv_v, g * NB + n + 3)
                    pe.wait_ge(qt_a, g * FTN * NB + FTN * n + FTN + 2)
                    pe.wait_ge(att_v, g * NB + n + 1)
                    for k in range(2):
                        for f in range(FTN):
                            for b in range(2):
                                mm = pe.matmul(bank[4 + n % 2][64 * b:64 * b + 64, TOK * k:TOK * k + TOK],
                                               kvm[n % 2][:, k, FTN * b + f, :], qT[n % 2][:, f, TOK * b:TOK * b + TOK],
                                               start=(f == 0), stop=(f == FTN - 1))
                    mm.then_inc(at_p, 1)

                def project(r):
                    pe.wait_ge(att_v, g * NB + 2 * r + 4)
                    pe.wait_ge(lo_v, (g * Q + r) * 2) if r else None
                    pe.matmul(bank[6][:, 0:QC], wproj[:, :], attT[r % 2], start=True, stop=True).then_inc(pr_p, 1)

                def gates(r):
                    pe.wait_ge(xn_v, g * LN + Q + r + 1)
                    for t in range(4):
                        mm = pe.matmul(bank[6][0:TP, 2 * NE * t:2 * NE * t + 2 * NE], xn[r % 2][:, TP * t:TP * t + TP],
                                       gatew[:, :], start=True, stop=True)
                    mm.then_inc(gt_p, 1)

                def duplicate(r, b, dst):
                    for k in range(2):
                        mm = pe.matmul(dst[64 * k:64 * k + 64, 0:QC], ident[:, 64 * b:64 * b + 64], xn[r % 2],
                                       start=True, stop=True)
                    mm.then_inc(dup_p, 1)

                def dispatch_transposed(r):
                    pe.wait_ge(gt_v, (g * Q + r) * GTN + GTN)
                    pe.wait_ge(lo_v, (g * Q + r) * 2 + 1)
                    b16 = bank[7].bitcast(BF16)
                    for t in range(4):
                        mm = pe.transpose(b16[0:96, TP * t:TP * t + TP],
                                          d3[:, r % 2, 2 * t:2 * t + 2, :].rearrange("p b e -> p (b e)"),
                                          identb[0:TP, 0:TP])
                    mm.then_inc(dt_p, 1)

                pe.wait_ge(later_in, LATER)
                pe.wait_ge(pooled, g * 3 + 3)
                center(0, 0, bank[4])
                for r in range(Q):
                    if r + 1 < Q:
                        pe.wait_ge(xn_v, g * LN + r) if r else None
                        center(r + 1, r + 1, bank[4 + (r + 1) % 2])
                    variance(r, r, bank[6 + r % 2])
                    if r:
                        project_qkv(r - 1)
                project_qkv(Q - 1)
                pe.wait_ge(qkv_v, g * TILES + TILES + 4)
                pe.wait_ge(ones_g, g + 1)
                moments(0)
                q_features(0)
                for n in range(NB + 2):
                    r, odd = divmod(n - 2, 2)
                    if n + 1 < NB:
                        moments(n + 1)
                    if r >= 0 and not odd:
                        dispatch_transposed(r - 1) if r else None
                        project(r)
                    elif r >= 0:
                        gates(r)
                        duplicate(r, 0, bank[7])
                    if n + 1 < NB:
                        q_features(n + 1)
                    if r >= 0 and not odd:
                        pe.wait_ge(pr_v, g * Q + r + 1)
                        pe.wait_ge(dt_a, g * Q + r) if r else None
                        center(r, Q + r, bank[7])
                    elif r >= 0:
                        pe.wait_ge(gt_v, (g * Q + r) * GTN + 1)
                        duplicate(r, 1, bank[6])
                    if n < NB:
                        attend(n)
                    if r >= 0 and not odd:
                        variance(r, Q + r, bank[6])
                dispatch_transposed(Q - 1)

            def experts(g):
                pe.wait_ge(split_v, 2)
                pe.wait_ge(lo_v, (g + 1) * 2 * Q)
                wait_alone(pe, dt_a, g * Q + Q)
                with pe.Fori(0, FCH) as j:
                    step0 = (g * FCH + j) * FF

                    xj = [xs[:, b, bass.ds(j * 2 * TOK, 2 * TOK)] for b in range(2)]
                    dj = d3T[:, bass.ds(j * 2 * TOK, 2 * TOK)]

                    def up(e, b, hi, lo, dst, signal):
                        cols = slice(HID * e, HID * e + HID)
                        pe.matmul(dst, hi[:, cols], xj[b], start=True, stop=False)
                        pe.matmul(dst, lo[:, cols], xj[b], start=False, stop=True).then_inc(signal, 1)

                    def down(e):
                        for b in range(2):
                            i = 2 * e + b
                            pe.wait_ge(hid_v, step0 + i + 3)
                            pe.matmul(bank[6][64 * b:64 * b + 64, 0:2 * TOK], w3[:, e, :], hidT[i % 4],
                                      start=(e == 0), stop=(e == NE - 1)).then_inc(down_p, 1)

                    for e in range(NE):
                        for b in range(2):
                            pe.wait_ge(silu_a, step0 + 2 * e + b + 1)
                            up(e, b, w1h, w1l, bank[b][:, 0:2 * TOK], h1_p)
                        for b in range(2):
                            pe.wait_ge(sd_v, step0 + 2 * e + b + 1)
                            c = NE * b + e
                            pe.matmul(bank[4 + b][:, 0:2 * TOK], dsel[:, c:c + 1].to_broadcast([96, 128]), dj,
                                      start=True, stop=True).then_inc(dw_p, 1)
                        for b in range(2):
                            pe.wait_ge(hid_v, step0 + 2 * e + b + 1)
                            up(e, b, w2h, w2l, bank[2 + b][:, 0:2 * TOK], h2_p)
                        if e == 1:
                            pe.wait_ge(out_v, g * FCH + j + 1)
                        if e:
                            down(e - 1)
                    down(NE - 1)

            pe.wait_ge(params_in, PARAMS)
            pe.wait_ge(setup_v, SETUP_V)
            with pe.Fori(0, GROUPS) as g:
                pe.wait_ge(out_v, g * FCH + 1)
                for l in range(S):
                    scan_layer(g, l)
                attention(g)
                experts(g)

        @block.scalar
        def _(act):
            for i in range(S):
                act.sem_inc(evac[i], 2)
                act.sem_inc(seld[i], 1)
                act.sem_inc(decay[i], 2)
            act.sem_inc(qt_a, 2)
            act.sem_inc(silu_a, 2)

            def scan_layer(g, l):
                n, w, U = NC[l], CW[l], KU[l]
                act.preload_act_table_set("natural_log_exp_and_others")
                with act.Fori(0, n // 2) as i:
                    for k in range(2):
                        c = i * 2 + k
                        act.wait_ge(proj[l], g * n + c + 1)
                        act.wait_ge(dlt[l], g * n + c + 1)
                        act.activation(eT[k][:, 0:w], bank[4 + k][:, 0:w], ACT.Abs, bias=bdt[:, l:l + 1])\
                            .then_inc(absd[l], 1)
                        act.activation(col(Bn, c, w), bank[k][:, 0:w], ACT.Copy)
                        act.activation(col(Cn, c, w), bank[2 + k][:, 0:w], ACT.Copy).then_inc(evac[l], 1)
                        act.wait_ge(absd[l], g * n + c + 1)
                        act.activation(eT[k][:, 0:w], eT[k][:, 0:w], ACT.Exp, scale=-1.0).then_inc(expd[l], 1)
                        act.wait_ge(expd[l], g * n + c + 1)
                        act.activation(lT[k][:, 0:w], eT[k][:, 0:w], ACT.Ln, bias=1.0).then_inc(lnd[l], 1)
                act.wait_ge(dec_v[l], g * DECV + 10)
                wait_alone(act, y0[l], g * n + n)

                def work(s):
                    wait_alone(act, bcast[l], (g * NS + s) * U + U)
                    act.activation(sel, blocks[:, :], ACT.Copy, scale=onehot[:, bass.ds(s, 1)]).then_inc(seld[l], 1)
                    with act.Fori(0, U // 2) as i:
                        for k in range(2):
                            q = i * 2 + k
                            wait_alone(act, scan[l], ((g * NS + s) * U + q + 1) * STEP[l])
                            act.activation(dA[k][:, 0:2 * w], col(delta, q, 2 * w), ACT.Exp,
                                           scale=Aslot[:, bass.ds(s, 1)]).then_inc(decay[l], 1)

                def skip(s, m):
                    act.wait_ge(decay[l], (g * NS + s) * U + 2)
                    act.sem_inc(seld[l], m)
                    act.sem_inc(decay[l], m * U)

                over_slots(act, skip, work)

            def attention(g):
                def squares(r, m, src):
                    act.wait_ge(cen_p, g * LN + m + 1)
                    act.activation(sqT[r % 2], src[:, 0:QC], ACT.Square).then_inc(csq_a, 1)

                def deviation(r, m, src):
                    act.wait_ge(var_p, g * LN + m + 1)
                    act.activation(xn[r % 2], src[:, 0:QC], ACT.Ln, bias=eps[:, :]).then_inc(dev_a, 1)
                    act.wait_ge(dev_a, (g * LN + m) * 2 + 1)
                    act.activation(xn[r % 2], xn[r % 2], ACT.Exp, scale=-0.5).then_inc(dev_a, 1)

                def qk_squares(r):
                    act.wait_ge(qkv_v, g * TILES + 4 * r + 8)
                    act.wait_ge(nrm_v, (g * Q + r - 1) * NRV + 1) if r else None
                    act.activation(sq.rearrange("p (u k c) -> p u k c", k=2, c=64),
                                   qkv[:, QU * r:QU * r + QU, 0:144].rearrange("p u (k c) -> p u k c", k=2)[:, :, :, 0:64],
                                   ACT.Square).then_inc(nrm_a, 1)

                def qk_norms(r):
                    act.wait_ge(nrm_v, (g * Q + r) * NRV + 2)
                    act.activation(norm[r], norm[r], ACT.Ln).then_inc(nrm_a, 1)
                    act.wait_ge(nrm_a, (g * Q + r) * NRA + 2)
                    act.activation(norm[r], norm[r], ACT.Exp, scale=-0.5).then_inc(nrm_a, 1)

                def linear(r):
                    act.wait_ge(nrm_v, (g * Q + r) * NRV + NRV)
                    act.wait_ge(ones_g, g + 1)
                    units = slice(QU * r, QU * r + QU)
                    act.wait_ge(qt_p, (g * NB + 2 * r - 2) * FTN) if r > 1 else None
                    act.activation(qF[r % 2][:, :, QUAD:FEATS], qkv[:, units, 0:72], ACT.Copy).then_inc(lin_a, 1)
                    act.wait_ge(kv_p, g * NB + 2 * r - 2) if r > 1 else None
                    act.activation(kF[r % 2][:, :, QUAD:FEATS], qkv[:, units, 72:144], ACT.Copy).then_inc(lin_a, 1)

                def q_features(n):
                    act.wait_ge(at_p, g * NB + n + 1)
                    for f in range(FTN):
                        t = FTN * n + f
                        act.wait_ge(qt_p, g * FTN * NB + t + 1)
                        act.activation(qT[n % 2][:, f, :], bank[2 + t % 2][0:FT, 0:QC], ACT.Copy).then_inc(qt_a, 1)

                def reciprocal(n):
                    r = n // 2
                    act.wait_ge(pr_p, g * Q + r - 1) if r > 1 else None
                    act.wait_ge(at_p, g * NB + n + 3)
                    dst = attT[r % 2][:, TOK * (n % 2):TOK * (n % 2) + TOK]
                    act.activation(dst, bank[4 + n % 2][:, TOK:2 * TOK], ACT.Ln).then_inc(rec_a, 1)
                    act.wait_ge(rec_a, (g * NB + n) * 2 + 1)
                    act.activation(dst, dst, ACT.Exp, scale=-1.0).then_inc(rec_a, 1)

                def high(r, b, src):
                    act.wait_ge(dup_p, (g * Q + r) * 2 + b + 1)
                    act.activation(xs[:, b, QC * r:QC * r + QC], src[:, 0:QC], ACT.Copy).then_inc(hi_a, 1)

                def dispatch_transposed(r):
                    act.wait_ge(dt_p, g * Q + r + 1)
                    act.activation(d3T[:, QC * r:QC * r + QC], bank[7].bitcast(BF16)[0:96, 0:QC], ACT.Copy)\
                        .then_inc(dt_a, 1)

                squares(0, 0, bank[4])
                for r in range(Q):
                    if r + 1 < Q:
                        squares(r + 1, r + 1, bank[4 + (r + 1) % 2])
                    deviation(r, r, bank[6 + r % 2])
                    if r:
                        qk_squares(r - 1)
                        qk_norms(r - 1)
                    if r > 1:
                        linear(r - 2)
                q_features(0)
                for n in range(NB + 2):
                    r, odd = divmod(n - 2, 2)
                    if r >= 0 and not odd:
                        dispatch_transposed(r - 1) if r else None
                    elif r >= 0:
                        high(r, 0, bank[7])
                    if n + 1 < NB:
                        q_features(n + 1)
                    if n == 1:
                        qk_norms(Q - 1)
                    if r >= 0 and not odd:
                        squares(r, Q + r, bank[7])
                    elif r >= 0:
                        act.wait_ge(gt_v, (g * Q + r) * GTN + 14)
                        act.activation(lg, lg, ACT.Exp).then_inc(gt_a, 1)
                        high(r, 1, bank[6])
                    if n < NB:
                        reciprocal(n)
                    if n == 0:
                        qk_squares(Q - 1)
                    if n in (1, 3):
                        linear(2 + n // 2)
                    if r >= 0 and not odd:
                        deviation(r, Q + r, bank[6])
                dispatch_transposed(Q - 1)

            def experts(g):
                act.preload_act_table(ACT.Silu)
                with act.Fori(0, FCH) as j:
                    step0 = (g * FCH + j) * FF
                    for i in range(FF):
                        act.wait_ge(h1_p, step0 + i + 1)
                        act.wait_ge(sd_v, step0 + i + 1)
                        act.activation(sT[i % 2], bank[i % 2][:, 0:2 * TOK], ACT.Silu).then_inc(silu_a, 1)

            act.wait_ge(zeroed, 1)
            for dst, src in first:
                act.dma_start(dst, src).then_inc(params_in, 16)
            act.wait_ge(params_in, PARAMS)
            act.wait_ge(setup_v, 1)
            act.activation(A[:, :, :], A[:, :, :], ACT.Exp).then_inc(setup_a, 1)
            act.activation(AT[:, :, :], AT[:, :, :], ACT.Exp).then_inc(setup_a, 1)
            with act.Fori(0, GROUPS) as g:
                for l in range(S):
                    scan_layer(g, l)
                attention(g)
                experts(g)

        @block.vector
        def _(v):
            for i in range(S):
                v.sem_inc(dlt[i], 2)
                v.sem_inc(relud[i], 2)
                v.sem_inc(ug[i], 2)
                v.sem_inc(scan[i], 2 * STEP[i])
                v.sem_inc(hc[i], 2)
            v.sem_inc(qkv_v, 4)
            v.sem_inc(kv_v, 2)
            v.sem_inc(att_v, 2)
            v.sem_inc(sd_v, 2)
            v.sem_inc(hid_v, 2)
            v.sem_inc(out_v, 1)

            def setup():
                v.memset(wB[:, :, :], 0.0)
                v.memset(wC[:, :, :], 0.0).then_inc(zeroed, 1)
                v.memset(wqkv[:, :], 0.0)
                v.memset(gatew[:, :], 0.0)
                v.memset(wproj[:, :], 0.0).then_inc(zeroed, 1)
                v.memset(wZ[:, :, :], 0.0)
                v.memset(resid[:, :], 0.0)
                v.memset(ones64[:, :], 1.0)
                v.memset(eps[:, :], LN_EPS)
                v.memset(fscale[:, 8:16], SCALE).then_inc(zeroed, 1)
                v.wait_ge(zeroed, 3)
                v.wait_ge(params_in, PARAMS)
                v.tensor_scalar(A[:, :, :], A[:, :, :], 88.0, None, ALU.min)
                v.tensor_scalar(AT[:, :, :], AT[:, :, :], 88.0, None, ALU.min).then_inc(setup_v, 1)
                v.tensor_scalar(wC[:, 0:2, :], wC[:, 0:2, :], 0.5, None, ALU.mult)
                v.tensor_scalar(dskip[:, 0:2], dskip[:, 0:2], 0.5, None, ALU.mult)
                v.tensor_scalar(fscale[:, 0:8], fscale[:, 0:8], SCALE, None, ALU.mult)
                v.tensor_copy(identb[:, :], ident[:, :])
                v.tensor_copy(dsel[:, :], dsel32)
                for l in range(S):
                    for k in range(2):
                        blk = slice(64 * k, 64 * k + 64)
                        v.tensor_scalar(wZ[blk, l, blk], wdt[blk, l, :], w0[blk, l:l + 1], None, ALU.mult)
                v.wait_ge(setup_a, 2)
                v.tensor_scalar(A[:, :, :], A[:, :, :], -1.0, None, ALU.mult)
                v.tensor_scalar(AT[:, :, :], AT[:, :, :], -1.0, None, ALU.mult).then_inc(setup_v, 1)

            def split_experts():
                v.wait_ge(staged, 64)
                v.tensor_copy(w1h[:, :], x0[:, 0:2048])
                v.tensor_copy(w2h[:, :], x0[:, 2048:4096]).then_inc(split_v, 1)
                v.wait_ge(split_v, 1)
                v.tensor_tensor(w1l[:, :], x0[:, 0:2048], w1h[:, :].bitcast(F32), ALU.subtract)
                v.tensor_tensor(w2l[:, :], x0[:, 2048:4096], w2h[:, :].bitcast(F32), ALU.subtract).then_inc(split_v, 1)

            def scan_layer(g, l):
                n, w, U, x = NC[l], CW[l], KU[l], xl[l]
                with v.Fori(0, n // 2) as i:
                    for k in range(2):
                        c = i * 2 + k
                        v.wait_ge(absd[l], g * n + c + 1)
                        v.tensor_scalar(rT[k][:, 0:w], bank[4 + k][:, 0:w], bdt[:, l:l + 1], 0.0, ALU.add, ALU.max)\
                            .then_inc(relud[l], 1)
                        v.wait_ge(onep[l], g * n + c + 1)
                        e, t = eT[k][:, 0:w], uT[k][:, 0:w]
                        v.scalar_tensor_tensor(t, t, 1.0, e, ALU.subtract, ALU.subtract, reverse1=True)\
                            .then_inc(corr[l], 1)
                        v.wait_ge(corr[l], g * n + c + 1)
                        v.wait_ge(wsum[l], g * n + c + 1)
                        v.tensor_tensor(col(delta, c, w), t, lT[k][:, 0:w], ALU.add).then_inc(dlt[l], 1)
                        v.wait_ge(dlt[l], g * n + c + 3)
                        v.tensor_reduce(mins[:, bass.ds(c, 1)], col(delta, c, w), AXX, ALU.min)
                        v.tensor_tensor(col(u, c, w), col(delta, c, w), col(x, c, w), ALU.mult).then_inc(udone[l], 1)

                step = [0]

                def then(ins, last=True):
                    if last:
                        step[0] += 1
                        ins.then_inc(dec_v[l], 1)
                        v.wait_ge(dec_v[l], g * DECV + step[0])

                v.wait_ge(udone[l], g * n + n)
                then(v.tensor_reduce(minall[:, :], mins[:, 0:n], AXX, ALU.min))
                v.tensor_scalar(amax2[:, 0, :], A[:, l, :], minall[:, :], None, ALU.mult)
                then(v.tensor_scalar(amax2[:, 1, :], A[:, l, :], minall[:, :], None, ALU.mult))
                v.wait_ge(dec_p[l], g * DECP + 1)
                then(v.tensor_reduce(amx[:, :], bank[6][:, 0:128], AXX, ALU.max))
                then(v.tensor_scalar(fast[:, :], amx[:, :], EXP_ZERO, None, ALU.is_le))
                then(v.tensor_scalar(slow[:, :], fast[:, :], -1.0, 1.0, ALU.mult, ALU.add))
                then(v.tensor_scalar(fastblk[:, :], blocks[:, :], fast[:, :], None, ALU.mult))
                v.wait_ge(dec_p[l], g * DECP + 2)
                then(v.tensor_copy(rank[:, :], bank[6][:, 128:129]))
                then(v.tensor_copy(count[:, :], bank[6][0:1, 130:131]))
                then(v.tensor_scalar(onehot[:, :], slotno[:, :], rank[:, :], slow[:, :], ALU.is_equal, ALU.mult))
                v.wait_ge(dec_p[l], g * DECP + 3)
                v.tensor_copy(Aslot[:, :], bank[6][:, 256:256 + NS]).then_inc(dec_v[l], 1)
                assert step[0] == DECV - 1

                with v.Fori(0, n // 2) as i:
                    for k in range(2):
                        c = i * 2 + k
                        v.wait_ge(gsum[l], g * n + c + 3)
                        v.tensor_tensor(gT[k][:, 0:w], bank[6 + k][:, 0:w], col(u, c, w), ALU.mult).then_inc(ug[l], 1)
                        v.wait_ge(ug[l], g * n + c + 3)
                        v.scalar_tensor_tensor(col(x, c, w), col(x, c, w), dskip[:, l:l + 1], gT[k][:, 0:w],
                                               ALU.mult, ALU.add).then_inc(y0[l], 1)

                def work(s):
                    with v.Fori(0, U // 2) as i:
                        for k in range(2):
                            q = i * 2 + k
                            unit = (g * NS + s) * U + q
                            h = hT[k]
                            v.wait_ge(bcast[l], unit + 1 + U)
                            bu = pairs[k][:, :, 0:w]
                            v.tensor_tensor(bu, bu, col(u, q, 2 * w).rearrange("p (b t) -> p b t", b=2), ALU.mult)\
                                .then_inc(scan[l], 1)
                            v.wait_ge(decay[l], unit + 3)
                            v.wait_ge(ysum[l], unit + 1)
                            parts = STEP[l] - 1
                            m = 2 * w // parts
                            for p in range(parts):
                                v.wait_ge(scan[l], (unit + 2) * STEP[l] + (1 + p if l == 0 else 1))
                                b, off = divmod(p * m, w)
                                first = h[:, p * m - 1:p * m] if l == 0 and p else 0.0
                                v.tensor_tensor_scan(h[:, p * m:p * m + m], dA[k][:, p * m:p * m + m],
                                                     pairs[k][:, b, off:off + m], first, ALU.mult, ALU.add)\
                                    .then_inc(scan[l], 1)
                            v.wait_ge(scan[l], (unit + 3) * STEP[l])
                            h2 = h[:, 0:2 * w].rearrange("p (b t) -> p b t", b=2)
                            v.tensor_tensor(h2, h2, pairs[2 + k][:, :, 0:w], ALU.mult).then_inc(hc[l], 1)

                def skip(s, m):
                    v.wait_ge(hc[l], (g * NS + s) * U + 2)
                    v.sem_inc(scan[l], m * U * STEP[l])
                    v.sem_inc(hc[l], m * U)

                over_slots(v, skip, work)
                v.wait_ge(ysum[l], (g + 1) * NS * U + 2)
                v.wait_ge(y0[l], g * n + n)
                if l < S - 1:
                    L2 = LEN[l + 1]
                    y = x.rearrange("p (b t) -> p b t", b=NB)[:, :, 0:2 * L2].rearrange("p b (t k) -> p b t k", k=2)
                    v.tensor_tensor(xl[l + 1].rearrange("p (b t) -> p b t", b=NB), y[:, :, :, 0], y[:, :, :, 1], ALU.add)\
                        .then_inc(pooled, 1)
                else:
                    v.wait_ge(out_d, g * FCH * 16 + 16)
                    v.tensor_copy(resid[:, :].rearrange("p (b t) -> p b t", b=NB)[:, :, 0:NT],
                                  x.rearrange("p (b t) -> p b t", b=NB)).then_inc(pooled, 1)

            def bc(t, m):
                return t.unsqueeze(len(t.shape)).to_broadcast(list(t.shape) + [m])

            def over(t, m, at):
                shape = list(t.shape)
                shape.insert(at, m)
                return t.unsqueeze(at).to_broadcast(shape)

            def attention(g):
                def normalize(r, m, src):
                    v.wait_ge(dev_a, (g * LN + m) * 2 + 2)
                    v.tensor_tensor(xn[r % 2], src[:, 0:QC], xn[r % 2], ALU.mult).then_inc(xn_v, 1)

                def qkv_bias(r):
                    for i in range(4 * r, 4 * r + 4):
                        v.wait_ge(qkv_p, g * TILES + i + 1)
                        dst = qkv[:, 2 * i:2 * i + 2, :].rearrange("p b (k c) -> p b k c", c=72)[:, :, :, 0:64]
                        v.tensor_tensor(dst, bank[i % 4][0:TP, 0:384].rearrange("p (b k c) -> p b k c", b=2, k=3),
                                        bqkv[0:TP, :].rearrange("p (b k c) -> p b k c", b=2, k=3), ALU.add)\
                            .then_inc(qkv_v, 1)

                def norm_step(r, i, ins):
                    ins.then_inc(nrm_v, 1)
                    v.wait_ge(nrm_v, (g * Q + r) * NRV + i)

                def qk_sums(r):
                    v.wait_ge(nrm_a, (g * Q + r) * NRA + 1)
                    norm_step(r, 1, v.tensor_reduce(norm[r].rearrange("p u h -> p (u h)"),
                                                    sq.rearrange("p (n d) -> p n d", d=D), AXX, ALU.add))
                    norm_step(r, 2, v.tensor_tensor(norm[r], norm[r], over(floor[0:TP, :], QU, 1), ALU.max))

                def heads(r, at):
                    return qkv[:, QU * r:QU * r + QU, at:at + 64].rearrange("p u (h d) -> p u h d", d=D)

                def qk_scale(r):
                    v.wait_ge(nrm_a, (g * Q + r) * NRA + 3)
                    norm_step(r, 3, v.tensor_tensor(norm[r], norm[r], over(fscale[0:TP, :], QU, 1), ALU.mult))
                    norm_step(r, 4, v.tensor_tensor(heads(r, 72), heads(r, 72), bc(norm[r][:, :, 8:16], D), ALU.mult))
                    norm_step(r, 5, v.tensor_tensor(heads(r, 0), heads(r, 0), bc(norm[r][:, :, 0:8], D), ALU.mult))

                def q_products(r):
                    v.wait_ge(qt_p, (g * NB + 2 * r - 2) * FTN) if r > 1 else None
                    products(v, qF[r % 2], heads(r, 0)).then_inc(qf_v, 1)

                def moments(n):
                    v.wait_ge(kv_p, g * NB + n + 1)
                    v.wait_ge(at_p, g * NB + n + 1)
                    src = bank[n % 2][0:FT, 0:2 * FTN * 65].rearrange("p (f c) -> p f c", c=65)
                    v.tensor_tensor(kvm[n % 2][:, 0], src[:, :, 1:65], featw[:, :, :], ALU.mult)
                    v.tensor_tensor(kvm[n % 2][:, 1], src[:, :, 0:1].to_broadcast([FT, 2 * FTN, 64]), featw[:, :, :],
                                    ALU.mult).then_inc(kv_v, 1)

                def attend(n):
                    v.wait_ge(rec_a, (g * NB + n) * 2 + 2)
                    dst = attT[n // 2 % 2][:, TOK * (n % 2):TOK * (n % 2) + TOK]
                    v.tensor_tensor(dst, bank[4 + n % 2][:, 0:TOK], dst, ALU.mult).then_inc(att_v, 1)

                def low(r, b, src):
                    v.wait_ge(hi_a, (g * Q + r) * 2 + b + 1)
                    dst = xs[64:128, b, QC * r:QC * r + QC]
                    v.tensor_tensor(dst, src[64:128, 0:QC], dst.bitcast(F32), ALU.subtract).then_inc(lo_v, 1)

                v.wait_ge(later_in, LATER)
                normalize(0, 0, bank[4])
                for r in range(1, Q + 1):
                    if r < Q:
                        normalize(r, r, bank[4 + r % 2])
                    qkv_bias(r - 1)
                    if r > 1:
                        qk_scale(r - 2)
                    if r < Q:
                        qk_sums(r - 1)
                    if r == Q - 1:
                        q_products(0)
                moments(0)
                for n in range(NB + 2):
                    r, odd = divmod(n - 2, 2)
                    if n + 1 < NB:
                        moments(n + 1)
                    if r >= 0 and not odd:
                        v.wait_ge(pr_p, g * Q + r + 1)
                        x = resid[:, QC * r:QC * r + QC]
                        v.scalar_tensor_tensor(x, bank[6][:, 0:QC], bproj[:, :], x, ALU.add, ALU.add).then_inc(pr_v, 1)
                    elif r >= 0:
                        gating(g, r)
                        low(r, 0, bank[7])
                    if n < NB:
                        attend(n)
                    if n == 0:
                        qk_sums(Q - 1)
                        q_products(1)
                    if n == 1:
                        qk_scale(Q - 1)
                    if r >= 0 and not odd:
                        normalize(r, Q + r, bank[7])
                    elif r >= 0:
                        low(r, 1, bank[6])
                    if n in (2, 4):
                        q_products(1 + n // 2)

            def gating(g, r):
                step = [0]

                def then(ins):
                    step[0] += 1
                    ins.then_inc(gt_v, 1)
                    v.wait_ge(gt_v, (g * Q + r) * GTN + step[0])

                m1, first, m2, den = (small[:, k, :] for k in range(4))
                d = d3[:, r % 2]
                v.wait_ge(gt_p, g * Q + r + 1)
                then(v.tensor_tensor(lg, bank[6][0:TP, 0:QU * NE].rearrange("p (u e) -> p u e", e=NE),
                                     over(gateb[0:TP, :], QU, 1), ALU.add))
                then(v.tensor_reduce(m1, lg, AXX, ALU.max))

                def first_of(src, top, dst):
                    then(v.tensor_tensor(eq, src, bc(top, NE), ALU.is_equal))
                    then(v.tensor_tensor(eq, eq, over(ridx[0:TP, :], QU, 1), ALU.mult))
                    then(v.tensor_reduce(first, eq, AXX, ALU.max))
                    then(v.tensor_tensor(dst, eq, bc(first, NE), ALU.is_equal))

                first_of(lg, m1, mask)
                then(v.scalar_tensor_tensor(rest, mask, BIG_NEG, lg, ALU.mult, ALU.add))
                then(v.tensor_reduce(m2, rest, AXX, ALU.max))
                first_of(rest, m2, mask2)
                then(v.tensor_tensor(mask, mask, mask2, ALU.add))
                then(v.tensor_tensor(lg, lg, bc(m1, NE), ALU.subtract))
                v.wait_ge(gt_a, g * Q + r + 1)
                then(v.tensor_tensor(lg, lg, mask, ALU.mult))
                then(v.tensor_reduce(den, lg, AXX, ALU.add))
                then(v.reciprocal(den, den))
                then(v.tensor_tensor(lg, lg, bc(den, NE), ALU.mult))
                then(v.tensor_copy(d[:, :, 0:16], lg))
                then(v.tensor_tensor(lg, lg, d[:, :, 0:16], ALU.subtract))
                then(v.tensor_copy(d[:, :, 16:32], lg))
                then(v.tensor_tensor(lg, lg, d[:, :, 16:32], ALU.subtract))
                then(v.tensor_copy(d[:, :, 32:48], lg))
                assert step[0] == GTN

            def experts(g):
                with v.Fori(0, FCH) as j:
                    step0 = (g * FCH + j) * FF
                    for i in range(FF):
                        k = i % 2
                        v.wait_ge(silu_a, step0 + i + 3)
                        v.wait_ge(dw_p, step0 + i + 1)
                        v.tensor_tensor(tT[k], bank[4 + k][:, 0:2 * TOK], sT[k], ALU.mult).then_inc(sd_v, 1)
                        v.wait_ge(sd_v, step0 + i + 3)
                        v.wait_ge(h2_p, step0 + i + 1)
                        v.wait_ge(down_p, step0 + i + 1)
                        v.tensor_tensor(hidT[i % 4], bank[2 + k][:, 0:2 * TOK], tT[k], ALU.mult).then_inc(hid_v, 1)
                    v.wait_ge(down_p, step0 + FF + 4)
                    r = resid[:, bass.ds(j * 2 * TOK, 2 * TOK)]
                    v.tensor_tensor(r, bank[6][:, 0:2 * TOK], r, ALU.add).then_inc(out_v, 1)

            setup()
            with v.Fori(0, GROUPS) as g:
                for l in range(S):
                    scan_layer(g, l)
                    if l == 1:
                        with v.If(g < 1):
                            split_experts()
                        with v.Else():
                            v.nop()
                attention(g)
                experts(g)

        @block.gpsimd
        def _(pool):
            for i in range(S):
                pool.sem_inc(ysum[i], 2)

            def scan_layer(g, l):
                n, w, U, x = NC[l], CW[l], KU[l], xl[l]
                with pool.Fori(0, n // 2) as i:
                    for k in range(2):
                        c = i * 2 + k
                        wait_alone(pool, expd[l], g * n + c + 1)
                        pool.tensor_scalar(uT[k][:, 0:w], eT[k][:, 0:w], 1.0, 1.0, ALU.mult, ALU.add).then_inc(onep[l], 1)
                        pool.wait_ge(relud[l], g * n + c + 3)
                        pool.wait_ge(lnd[l], g * n + c + 1)
                        pool.tensor_tensor(lT[k][:, 0:w], lT[k][:, 0:w], rT[k][:, 0:w], ALU.add).then_inc(wsum[l], 1)
                wait_alone(pool, dlt[l], g * n + n + 2)
                with pool.Fori(0, n // 2) as i:
                    for k in range(2):
                        c = i * 2 + k
                        pool.wait_ge(gsum[l], g * n + c + 1)
                        pool.tensor_tensor(bcT[k][:, 0:w], col(Bn, c, w), col(Cn, c, w), ALU.mult).then_inc(bcd[l], 1)
                wait_alone(pool, dec_v[l], g * DECV + 10)

                def work(s):
                    with pool.Fori(0, U // 2) as i:
                        for k in range(2):
                            q = i * 2 + k
                            unit = (g * NS + s) * U + q
                            pool.wait_ge(hc[l], unit + 3)
                            pool.wait_ge(ysum[l], unit + 2)
                            y = col(x, q, 2 * w)
                            pool.tensor_tensor(y, y, hT[k][:, 0:2 * w], ALU.add).then_inc(ysum[l], 1)

                def skip(s, m):
                    pool.wait_ge(ysum[l], (g * NS + s) * U + 2)
                    pool.sem_inc(ysum[l], m * U)

                over_slots(pool, skip, work)

            def attention(g):
                wait_alone(pool, pooled, g * 3 + 3)
                pool.memset(qkv[:, :, 64:72], 1.0)
                pool.memset(qkv[:, :, 136:144], 1.0).then_inc(ones_g, 1)
                for r in range(Q):
                    k4 = qkv[:, QU * r:QU * r + QU, 72:136].rearrange("p u (h d) -> p u h d", d=D)
                    pool.wait_ge(nrm_v, (g * Q + r) * NRV + 4)
                    if r > 1:
                        pool.wait_ge(kv_p, g * NB + 2 * r - 2)
                    products(pool, kF[r % 2], k4).then_inc(kf_g, 1)

            with pool.Fori(0, GROUPS) as g:
                for l in range(S):
                    scan_layer(g, l)
                attention(g)


def products(eng, dst, t):
    at = 0
    for k in range(D):
        m = D - k
        ins = eng.tensor_tensor(dst[:, :, at:at + H * m].rearrange("p u (h d) -> p u h d", d=m),
                                t[:, :, :, 0:m], t[:, :, :, k:D], ALU.mult)
        at += H * m
    return ins



def shape_constants():
    import numpy as np
    f = np.float32
    half = np.arange(128) // 64
    featw = np.zeros((FEATS, 64), f)
    scale2 = D ** 0.5

    def put(row, head, weight):
        featw[row, 8 * head:8 * head + 8] = weight

    row = 0
    for k in range(D):
        for head in range(H):
            for _ in range(D - k):
                put(row, head, 0.5 if k == 0 else 1.0)
                row += 1
    for i in range(64):
        put(QUAD + i, i // D, scale2)
    for head in range(H):
        put(QUAD + 64 + head, head, scale2 * scale2)
    dsel = np.zeros((2, 3, NE, 2 * NE), f)
    for b in range(2):
        for e in range(NE):
            dsel[b, :, e, NE * b + e] = 1
    n = np.arange(64)
    tri = np.zeros((128, 128), f)
    tri[:64] = np.tile((n[:, None] < n[None, :]).astype(f), (1, 2))
    return {
        "ident": np.eye(128, dtype=f), "blocks": (half[:, None] == half[None, :]).astype(f), "tri": tri,
        "slotno": np.tile(np.arange(NS, dtype=f), (128, 1)), "ridx": np.tile(np.arange(NE, 0, -1, dtype=f), (128, 1)),
        "featw": np.tile(featw.reshape(FTN, FT, 64).transpose(1, 0, 2), (1, 2, 1)),
        "dsel": dsel.reshape(6 * NE, 2 * NE),
        "floor": np.tile(np.array([NORM_EPS ** 2 / D ** 0.5] * 8 + [NORM_EPS ** 2] * 8, f), (128, 1)),
        "averaging": (half[:, None] == half[None, :]).astype(f) / 64,
        "centering": np.eye(128, dtype=f) - (half[:, None] == half[None, :]).astype(f) / 64,
    }


def laid_out(i):
    import numpy as np
    i = {k: np.asarray(x) for k, x in i.items()}

    def rows(x, n=128):
        return np.tile(x.reshape(1, -1), (n, 1))

    x = i["x"].reshape(2, 16, SEQ, C).transpose(0, 3, 1, 2)
    w = i["L0_tok_W_dbc"].transpose(2, 0, 1)
    alog = i["L0_tok_A_log"]
    a = {
        "x": x.reshape(128, GROUPS, NB * SEQ),
        "w_tok": w, "w_tok0": w[:, :, 0],
        "wdt": rows(i["L0_tok_W_dt"]).reshape(128, LAYERS, 64),
        "alog": np.tile(alog.transpose(1, 0, 2), (2, 1, 1)),
        "alogT": np.tile(alog.transpose(2, 0, 1), (1, 1, 2)),
        "dskip": np.tile(i["L0_tok_D"].T, (2, 1)), "bdt": np.tile(i["L0_tok_b_dt"].T, (2, 1)),
        "wqkv": i["L0_attn_Wqkv"].T, "bqkv": rows(np.tile(i["L0_attn_bqkv"], 2)),
        "wproj": i["L0_attn_Wproj"].T, "bproj": np.tile(i["L0_attn_bproj"][:, None], (2, 1)),
        "temp": rows(i["L0_attn_temperature"]), "gate_w": i["L0_ffn_gate_w"], "gate_b": rows(i["L0_ffn_gate_b"]),
        "w1": i["L0_ffn_w1"].transpose(1, 0, 2).reshape(64, NE * HID),
        "w2": i["L0_ffn_w2"].transpose(1, 0, 2).reshape(64, NE * HID),
        "w3": i["L0_ffn_w3"].transpose(1, 0, 2),
    }
    return {k: np.ascontiguousarray(x) for k, x in (a | shape_constants()).items()}


def kernel(**inputs):
    import numpy as np
    import concourse.bacc as bacc
    from concourse.bass_utils import run_bass_kernel_spmd

    nc = bacc.Bacc("TRN2", target_bir_lowering=False, num_devices=1)
    arrays = {f"in_{k}": x for k, x in laid_out(inputs).items()}
    a = {k[3:]: nc.dram_tensor(k, x.shape, mybir.dt.from_np(x.dtype), kind="ExternalInput").ap()
         for k, x in arrays.items()}
    out = nc.dram_tensor("out", (128, 16, NT), F32, kind="ExternalOutput").ap()
    program(nc, a, out)
    r = run_bass_kernel_spmd(nc, [arrays], core_ids=[0])
    y = np.asarray(r.results[0]["out"]).reshape(2, C, 16, NT)
    return np.ascontiguousarray(y.transpose(0, 2, 3, 1)).reshape(BATCH, NT, C)
```

```python
from contextlib import ExitStack

import concourse.bass as bass
from concourse import mybir

ALU = mybir.AluOpType
ACT = mybir.ActivationFunctionType
AXX = mybir.AxisListType.X
F32 = mybir.dt.float32
F32R = mybir.dt.float32r
BF16 = mybir.dt.bfloat16
I32 = mybir.dt.int32

BATCH, SEQ, C = 32, 750, 64
GROUPS, NB = 2, 8
NS = 64
LAYERS = 3
LEN = [750, 375, 187]
CW = [375, 375, 374]
NC = [16, 8, 4]
PEEL = 4
EXP_ZERO = -104.0
LN_EPS = 1e-5
H, D = 8, 8
NT = 187
TP = 94
TOK = 2 * TP
TILES = 2 * NB
QUARTERS = NB // 2
QC = 2 * TOK
QU = 8
QKVW = 216
SETUP_V = 2
NE, HID = 16, 128
QUAD = 288
FEATS = QUAD + 72
FT, FTN = 120, 3
NORM_EPS = 1e-12
PACK = [128, 128, 128, NS, H, LAYERS, LAYERS, LAYERS, LAYERS * 64, LAYERS * NS]
PACK_AT = [sum(PACK[:i]) for i in range(len(PACK))]
PACKED = sum(PACK)
BIG_NEG = -3.0e38


def program(nc, a, out):
    SCALE = float(D) ** 0.25
    with ExitStack() as ctx:
        def sb(name, shape, dt=F32):
            return ctx.enter_context(nc.sbuf_tensor(name, shape, dt))

        def sem(name):
            return ctx.enter_context(nc.semaphore(name))

        pairs = [ctx.enter_context(nc.psum_tensor(f"pair{i}", [128, 2, 512], F32)) for i in range(4)]
        bank = [pairs[i // 2][:, i % 2, :] for i in range(8)]

        x0 = sb("x0", [128, NB * SEQ])
        big = sb("big", [128, 24000])
        Bn, Cn = big[:, 0:6000], big[:, 6000:12000]
        delta, u = big[:, 12000:18000], big[:, 18000:24000]
        xl = [x0[:, :], big[:, 3000:6000], big[:, 9000:9000 + NB * 187]]
        tmp = sb("tmp", [128, 3256])
        resid = sb("resid", [128, NB * TOK])

        packed = sb("packed", [128, PACKED])
        ident, blocks, tri, slotno, temp, w0, bdt, dskip, wdt, A = (
            packed[:, at:at + n] for at, n in zip(PACK_AT, PACK))
        wdt, A = (t.rearrange("p (l n) -> p l n", l=LAYERS) for t in (wdt, A))
        identb = sb("identb", [128, 128], BF16)
        ridx = sb("ridx", [128, NE])
        featw = sb("featw", [FT, 2 * FTN, 64])
        dsel = sb("dsel", [96, NE, 128], BF16)
        wB = sb("wB", [128, LAYERS, 128])
        wC = sb("wC", [128, LAYERS, 128])
        wZ = sb("wZ", [128, LAYERS, 128])
        AT = sb("AT", [64, LAYERS, 128])
        wqkv = sb("wqkv", [128, 384])
        bqkv = sb("bqkv", [128, 384])
        wproj = sb("wproj", [128, 128])
        bproj = sb("bproj", [128, 1])
        centering = sb("centering", [128, 128])
        averaging = sb("averaging", [128, 128])
        eps = sb("eps", [128, 1])
        floor = sb("floor", [128, 16])
        fscale = sb("fscale", [128, 16])
        gatew = sb("gatew", [128, 2 * NE])
        gateb = sb("gateb", [128, NE])
        w1h = sb("w1h", [128, NE * HID], F32R)
        w1l = sb("w1l", [128, NE * HID], F32R)
        w2h = sb("w2h", [128, NE * HID], F32R)
        w2l = sb("w2l", [128, NE * HID], F32R)
        w3 = sb("w3", [128, NE, 64])
        xs = sb("xs", [128, 2, NB * TOK], F32R)
        d3T = sb("d3T", [96, NB * TOK], BF16)
        ones64 = sb("ones64", [64, 1])

        mins = sb("mins", [128, 16])
        minall = sb("minall", [128, 1])
        amax2 = tmp[:, 1500:1500 + 2 * NS].rearrange("p (a n) -> p a n", a=2)
        amx = sb("amx", [128, 1])
        fast = sb("fast", [128, 1])
        slow = sb("slow", [128, 1])
        rank = sb("rank", [128, 1])
        fastblk = sb("fastblk", [128, 128])
        onehot = sb("onehot", [128, NS])
        count = sb("count", [1, 1], I32)
        Aslot = sb("Aslot", [128, NS])

        def two(at, n):
            return [tmp[:, at + n * j:at + n * j + n] for j in range(2)]

        eT, rT, uT, lT = (two(750 * k, 375) for k in range(4))
        bcT, gT = two(0, 750), two(1500, 750)
        dA, hT = two(0, 750), two(1500, 750)
        sel = two(3000, 128)

        def pick(at, rows, n, count=2):
            return [big[0:rows, at + n * j:at + n * j + n] for j in range(count)]

        qF, kF = (([t.rearrange("p (u f) -> p u f", f=FEATS) for t in pick(at, TP, QU * FEATS)])
                  for at in (0, 12672))
        qkv = big[0:TP, 5760:5760 + 4 * QU * QKVW].rearrange("p (u w) -> p u w", w=QKVW)
        kvm = [t.rearrange("p (k f c) -> p k f c", k=2, c=64)
               for t in pick(18432, FT, 4 * FTN * 64)]
        qT = [t.rearrange("p (f c) -> p f c", c=QC) for t in pick(19968, FT, FTN * QC)]
        attT = pick(22224, 128, QC)
        norm = [t.rearrange("p (u h) -> p u h", h=16) for t in pick(22976, TP, QU * 16, QUARTERS)]
        sqT = two(0, QC)
        xn = pick(18432, 128, QC, QUARTERS) + 2 * two(2 * QC, QC)
        sq = tmp[0:TP, 4 * QC:4 * QC + QU * 128]
        lg, eq, mask, rest, mask2 = (tmp[0:TP, 2528 + 128 * k:2656 + 128 * k].rearrange(
            "p (u e) -> p u e", e=NE) for k in range(5))
        ex = sq[:, 0:QU * NE].rearrange("p (u e) -> p u e", e=NE)
        dispatchT = bank[6].bitcast(BF16)[0:96, 256:256 + QC]
        small = big[0:TP, 23488:23520].rearrange("p (k u) -> p k u", u=QU)
        d3 = big[0:TP, 23520:23904].bitcast(BF16).rearrange("p (k u e) -> p k u e", k=2, u=QU)
        sT = two(0, QC)
        wT = two(2 * QC, QC)
        mT = pick(16000, 128, QC)
        hidT = [tmp[:, QC * (4 + j):QC * (5 + j)] for j in range(4)]

        S = LAYERS
        waited = sem("waited")
        params_in = sem("params_in")
        later_in = sem("later_in")
        staged = sem("staged")
        split_v = sem("split_v")
        zeroed = sem("zeroed")
        setup_v = sem("setup_v")
        setup_a = sem("setup_a")
        x_in = [sem(f"x_in{i}") for i in range(4)]
        projz = [sem(f"projz{i}") for i in range(S)]
        proj = [sem(f"proj{i}") for i in range(S)]
        evac = [sem(f"evac{i}") for i in range(S)]
        absd = [sem(f"absd{i}") for i in range(S)]
        relud = [sem(f"relud{i}") for i in range(S)]
        expd = [sem(f"expd{i}") for i in range(S)]
        onep = [sem(f"onep{i}") for i in range(S)]
        lnd = [sem(f"lnd{i}") for i in range(S)]
        wsum = [sem(f"wsum{i}") for i in range(S)]
        corr = [sem(f"corr{i}") for i in range(S)]
        dlt = [sem(f"dlt{i}") for i in range(S)]
        udone = [sem(f"udone{i}") for i in range(S)]
        dec_v = [sem(f"dec_v{i}") for i in range(S)]
        dec_p = [sem(f"dec_p{i}") for i in range(S)]
        bcd = [sem(f"bcd{i}") for i in range(S)]
        gsum = [sem(f"gsum{i}") for i in range(S)]
        ug = [sem(f"ug{i}") for i in range(S)]
        y0 = [sem(f"y0{i}") for i in range(S)]
        seld = [sem(f"seld{i}") for i in range(S)]
        bcast = [sem(f"bcast{i}") for i in range(S)]
        decay = [sem(f"decay{i}") for i in range(S)]
        scan = [sem(f"scan{i}") for i in range(S)]
        hc = [sem(f"hc{i}") for i in range(S)]
        ysum = [sem(f"ysum{i}") for i in range(S)]
        pooled = sem("pooled")
        cen_p, var_p = sem("cen_p"), sem("var_p")
        csq_a, dev_a = sem("csq_a"), sem("dev_a")
        xn_v = sem("xn_v")
        qkv_p, qkv_v = sem("qkv_p"), sem("qkv_v")
        nrm_v, nrm_a = sem("nrm_v"), sem("nrm_a")
        qf_v, kf_g = sem("qf_v"), sem("kf_g")
        lin_a = sem("lin_a")
        ones_g = sem("ones_g")
        kv_p, kv_v = sem("kv_p"), sem("kv_v")
        qt_p, qt_a = sem("qt_p"), sem("qt_a")
        at_p = sem("at_p")
        rec_a = sem("rec_a")
        att_v = sem("att_v")
        pr_p, pr_v = sem("pr_p"), sem("pr_v")
        gt_p, gt_v, gt_a = sem("gt_p"), sem("gt_v"), sem("gt_a")
        dup_p = sem("dup_p")
        hi_a, lo_v = sem("hi_a"), sem("lo_v")
        dt_p, dt_a = sem("dt_p"), sem("dt_a")
        h1_p, h2_p = sem("h1_p"), sem("h2_p")
        silu_a = sem("silu_a")
        dw_p = sem("dw_p")
        dw_a = sem("dw_a")
        hid_v = sem("hid_v")
        down_p = sem("down_p")
        mix_v = sem("mix_v")
        add_g = sem("add_g")
        out_d = sem("out_d")

        first, later = [], []
        for k in range(2):
            blk = slice(64 * k, 64 * k + 64)
            first += [(wB[blk, :, blk], a["w_tok"][:, :, 1:65]), (wC[blk, :, blk], a["w_tok"][:, :, 65:129])]
            later += [(wqkv[blk, 192 * k:192 * k + 192], a["wqkv"]), (wproj[blk, blk], a["wproj"]),
                      (gatew[blk, NE * k:NE * k + NE], a["gate_w"])]
        first += [(packed[:, :], a["packed"]), (AT[:, :, :], a["alogT"])]
        later += [(t[:, :], a[n]) for t, n in (
            (bqkv, "bqkv"), (bproj, "bproj"), (gateb, "gate_b"), (floor, "floor"), (ridx, "ridx"),
            (centering, "centering"), (averaging, "averaging"))]
        later += [(featw[:, :, :], a["featw"]), (w3[:, :, :], a["w3"])]
        PARAMS, LATER = 16 * len(first), 16 * len(later)

        KU = [n // 2 for n in NC]
        STEP = [3, 3, 5]
        PARTS = 4
        POOLED = 2 * PARTS + 1
        DECV, DECP = 8, 3
        Q, LN = QUARTERS, 2 * QUARTERS
        NRV, NRA, GTN = 5, 3, 22
        FF = NE * 2
        FCH = QUARTERS

        def col(t, c, w):
            return t[:, bass.ds(c * w, w)]

        def wait_alone(eng, sem, value):
            eng.wait_ge(sem, value)
            eng.sem_inc(waited, 1)

        def over_slots(eng, skip, work):
            n = eng.value_load(count[0:1, 0:1], min_val=0, max_val=NS)
            with eng.Fori(0, PEEL // 2) as i:
                for k in range(2):
                    s = i * 2 + k
                    with eng.If(n > s):
                        work(s, k)
                    with eng.Else():
                        skip(s, 1)
            with eng.If(n > PEEL):
                with eng.Fori(PEEL // 2, NS // 2) as i:
                    for k in range(2):
                        work(i * 2 + k, k)
            with eng.Else():
                skip(PEEL, NS - PEEL)
            eng.nop()

        block = ctx.enter_context(nc.Block())

        @block.sync
        def _(sp):
            sp.sem_inc(out_d, 16)
            def load(g, parts):
                for i in parts:
                    cols = slice(NB * SEQ // PARTS * i, NB * SEQ // PARTS * (i + 1))
                    sp.dma_start(x0[:, cols], a["x"][:, g, cols]).then_inc(x_in[i], 16)

            load(0, range(1))
            sp.wait_ge(params_in, PARAMS)
            load(0, range(1, PARTS))
            sp.wait_ge(zeroed, 2)
            for dst, src in later:
                sp.dma_start(dst, src).then_inc(later_in, 16)
            with sp.Fori(0, GROUPS) as g:
                with sp.If(g < 1):
                    sp.wait_ge(pooled, g * POOLED + PARTS)
                    for i, name in enumerate(("w1", "w2")):
                        for k in range(2):
                            sp.dma_start(x0[64 * k:64 * k + 64, 2048 * i:2048 * i + 2048], a[name]).then_inc(staged, 16)
                    sp.dma_start(x0[0:96, 4096:4096 + 2 * NE], a["dsel"]).then_inc(staged, 16)
                    sp.wait_ge(split_v, 2)
                with sp.Else():
                    sp.nop()
                with sp.If(g < GROUPS - 1):
                    sp.wait_ge(pooled, g * POOLED + PARTS)
                    load(1, range(PARTS))
                with sp.Else():
                    sp.nop()
                with sp.Fori(0, FCH) as j:
                    sp.wait_ge(add_g, (g * FCH + j + 1) * NE + 2)
                    sp.dma_start(out[:, bass.ds((g * FCH + j) * 2, 2), :],
                                 resid[:, bass.ds(j * QC, QC)].rearrange("p (b t) -> p b t", b=2)[:, :, 0:NT]
                                 ).then_inc(out_d, 16)
            sp.wait_ge(out_d, 16 * (FCH * GROUPS + 1))

        @block.tensor
        def _(pe):
            for i in range(S):
                pe.sem_inc(gsum[i], 2)
                pe.sem_inc(bcast[i], 2 * KU[i])
            pe.sem_inc(at_p, 2)
            pe.sem_inc(down_p, 2)

            def scan_layer(g, l):
                n, w, U, x = NC[l], CW[l], KU[l], xl[l]
                def project(i):
                    for k in range(2):
                        c = i * 2 + k
                        pe.wait_ge(relud[l], g * n + c + 1)
                        pe.matmul(bank[4 + k][:, 0:w], wZ[:, l, :], col(x, c, w), start=True, stop=True)\
                            .then_inc(projz[l], 1)
                        pe.wait_ge(evac[l], g * n + c + 1)
                        pe.matmul(bank[k][:, 0:w], wB[:, l, :], col(x, c, w), start=True, stop=True)
                        pe.matmul(bank[2 + k][:, 0:w], wC[:, l, :], col(x, c, w), start=True, stop=True)\
                            .then_inc(proj[l], 1)

                if l == 0:
                    for part in range(PARTS):
                        wait_alone(pe, x_in[part], g * 16 + 16)
                        with pe.Fori(n // 2 // PARTS * part, n // 2 // PARTS * (part + 1)) as i:
                            project(i)
                else:
                    m = PARTS * 2 // n
                    with pe.Fori(0, n // 2) as i:
                        wait_alone(pe, pooled, g * POOLED + i * m + (PARTS * (l - 1) + m))
                        project(i)
                pe.wait_ge(dec_v[l], g * DECV + 2)
                pe.transpose(bank[6][:, 0:128], amax2[:, :, :].rearrange("p a n -> p (a n)"), ident[:, :])\
                    .then_inc(dec_p[l], 1)
                pe.wait_ge(dec_v[l], g * DECV + 4)
                pe.matmul(bank[6][:, 128:129], tri[:, :], slow[:, :], start=True, stop=True)
                pe.matmul(bank[6][0:1, 130:131], slow[0:64, :], ones64[:, :], start=True, stop=True)\
                    .then_inc(dec_p[l], 1)
                def fast_sum(q, k):
                    pe.wait_ge(bcd[l], g * U + q + 1)
                    pe.wait_ge(ug[l], g * U + q + 1)
                    for b in range(2):
                        mm = pe.matmul(pairs[2 + k][:, b, 0:w], fastblk[:, :], bcT[k][:, w * b:w * b + w],
                                       start=True, stop=True)
                    mm.then_inc(gsum[l], 1)

                pe.wait_ge(dec_v[l], g * DECV + 5)
                fast_sum(0, 0)
                pe.wait_ge(dec_v[l], g * DECV + 7)
                pe.matmul(bank[6][:, 256:256 + NS], AT[:, l, :], onehot[0:64, :], start=True, stop=True)\
                    .then_inc(dec_p[l], 1)
                wait_alone(pe, dec_v[l], g * DECV + DECV)
                fast_sum(1, 1)
                if U > 2:
                    with pe.Fori(1, U // 2) as i:
                        for k in range(2):
                            fast_sum(i * 2 + k, k)
                wait_alone(pe, ug[l], g * U + U + 2)

                def work(s, j):
                    wait_alone(pe, seld[l], (g * NS + s) + 2)
                    with pe.Fori(0, U // 2) as i:
                        for k in range(2):
                            q = i * 2 + k
                            unit = (g * NS + s) * U + q
                            pe.wait_ge(scan[l], (unit + 1) * STEP[l])
                            for b in range(2):
                                pe.matmul(pairs[k][:, b, 0:w], sel[j], col(Bn, q * 2 + b, w), start=True, stop=True)
                            pe.wait_ge(hc[l], unit + 1)
                            for b in range(2):
                                mm = pe.matmul(pairs[2 + k][:, b, 0:w], sel[j], col(Cn, q * 2 + b, w), start=True, stop=True)
                            mm.then_inc(bcast[l], 1)

                def skip(s, m):
                    pe.wait_ge(bcast[l], (g * NS + s) * U + 2 * U)
                    pe.sem_inc(bcast[l], m * U)

                over_slots(pe, skip, work)

            def attention(g):
                def center(r, m, dst):
                    pe.matmul(dst[:, 0:QC], centering[:, :], resid[:, QC * r:QC * r + QC], start=True, stop=True)\
                        .then_inc(cen_p, 1)

                def variance(r, m, dst):
                    pe.wait_ge(csq_a, g * LN + m + 1)
                    pe.matmul(dst[:, 0:QC], averaging[:, :], sqT[r % 2], start=True, stop=True).then_inc(var_p, 1)

                def project_qkv(r):
                    for i in range(4 * r, 4 * r + 4):
                        pe.wait_ge(qkv_v, g * TILES + i + 1)
                        pe.matmul(bank[i % 4][0:TP, 0:384], xn[r][:, TP * (i % 4):TP * (i % 4) + TP], wqkv[:, :],
                                  start=True, stop=True).then_inc(qkv_p, 1)

                def moments(n):
                    r = n // 2
                    if n % 2 == 0:
                        pe.wait_ge(kf_g, g * Q + r + 1)
                        pe.wait_ge(lin_a, (g * Q + r) * 2 + 2)
                    pe.wait_ge(kv_v, g * NB + n + 1)
                    for b in range(2):
                        for f in range(FTN):
                            for p in range(2):
                                unit = (2 * n + p) * 2 + b
                                rows = TP - p
                                at = 65 * (FTN * b + f)
                                mm = pe.matmul(bank[n % 2][0:FT, at:at + 65],
                                               kF[r % 2][0:rows, unit % QU, FT * f:FT * f + FT],
                                               qkv[0:rows, unit, 143:208], start=(p == 0), stop=(p == 1))
                    mm.then_inc(kv_p, 1)

                def q_features(n):
                    r = n // 2
                    if n % 2 == 0:
                        pe.wait_ge(qf_v, g * Q + r + 1)
                    for f in range(FTN):
                        t = FTN * n + f
                        pe.wait_ge(qt_a, g * FTN * NB + t + 1)
                        for b in range(2):
                            for p in range(2):
                                at = TP * (2 * b + p)
                                mm = pe.transpose(bank[2 + t % 2][0:FT, at:at + TP],
                                                  qF[r % 2][:, ((2 * n + p) * 2 + b) % QU, FT * f:FT * f + FT],
                                                  ident[0:TP, 0:TP])
                        mm.then_inc(qt_p, 1)

                def attend(n):
                    pe.wait_ge(kv_v, g * NB + n + 3)
                    pe.wait_ge(qt_a, g * FTN * NB + FTN * n + FTN + 2)
                    pe.wait_ge(att_v, g * NB + n + 1)
                    for k in range(2):
                        for f in range(FTN):
                            for b in range(2):
                                mm = pe.matmul(bank[4 + n % 2][64 * b:64 * b + 64, TOK * k:TOK * k + TOK],
                                               kvm[n % 2][:, k, FTN * b + f, :], qT[n % 2][:, f, TOK * b:TOK * b + TOK],
                                               start=(f == 0), stop=(f == FTN - 1))
                    mm.then_inc(at_p, 1)

                def project(r):
                    pe.wait_ge(att_v, g * NB + 2 * r + 4)
                    pe.wait_ge(lo_v, (g * Q + r) * 2) if r else None
                    pe.matmul(bank[6][:, 0:QC], wproj[:, :], attT[r % 2], start=True, stop=True).then_inc(pr_p, 1)

                def gates(r):
                    for t in range(4):
                        mm = pe.matmul(bank[6][0:TP, 2 * NE * t:2 * NE * t + 2 * NE], xn[Q + r][:, TP * t:TP * t + TP],
                                       gatew[:, :], start=True, stop=True)
                    mm.then_inc(gt_p, 1)

                def duplicate(r, b, dst):
                    for k in range(2):
                        mm = pe.matmul(dst[64 * k:64 * k + 64, 0:QC], ident[:, 64 * b:64 * b + 64], xn[Q + r],
                                       start=True, stop=True)
                    mm.then_inc(dup_p, 1)

                def dispatch_transposed(r):
                    pe.wait_ge(gt_v, (g * Q + r) * GTN + GTN)
                    for t in range(4):
                        mm = pe.transpose(dispatchT[:, TP * t:TP * t + TP],
                                          d3[:, r % 2, 2 * t:2 * t + 2, :].rearrange("p b e -> p (b e)"),
                                          identb[0:TP, 0:TP])
                    mm.then_inc(dt_p, 1)

                pe.wait_ge(later_in, LATER)
                pe.wait_ge(pooled, g * POOLED + POOLED)
                for r in range(0, Q, 2):
                    for i in (r, r + 1):
                        pe.wait_ge(xn_v, g * LN + i - 1) if r else None
                        center(i, i, bank[4 + i % 2])
                    if r:
                        project_qkv(0)
                        project_qkv(1)
                    for i in (r, r + 1):
                        variance(i, i, bank[6 + i % 2])
                for r in (2, 3):
                    pe.wait_ge(xn_v, g * LN + r + 1)
                    project_qkv(r)
                pe.wait_ge(qkv_v, g * TILES + TILES + 4)
                pe.wait_ge(ones_g, g + 1)
                moments(0)
                q_features(0)
                for n in range(NB + 2):
                    r, odd = divmod(n - 2, 2)
                    if n + 1 < NB:
                        moments(n + 1)
                    if r >= 0 and not odd:
                        project(r)
                    elif r >= 0:
                        pe.wait_ge(xn_v, g * LN + Q + r + 1)
                        dispatch_transposed(r - 1) if r else None
                        gates(r)
                        duplicate(r, 0, bank[7])
                    if n + 1 < NB:
                        q_features(n + 1)
                    if r >= 0 and not odd:
                        pe.wait_ge(pr_v, g * Q + r + 1)
                        center(r, Q + r, bank[7])
                    elif r >= 0:
                        pe.wait_ge(gt_v, (g * Q + r) * GTN + 1)
                        pe.wait_ge(dt_a, g * Q + r) if r else None
                        duplicate(r, 1, bank[6])
                    if n < NB:
                        attend(n)
                    if r >= 0 and not odd:
                        variance(r, Q + r, bank[6])
                pe.wait_ge(lo_v, (g + 1) * 2 * Q)
                dispatch_transposed(Q - 1)

            def experts(g):
                pe.wait_ge(split_v, 2)
                wait_alone(pe, dt_a, g * Q + Q)
                with pe.Fori(0, FCH) as j:
                    step0 = (g * FCH + j) * FF
                    expert0 = (g * FCH + j) * NE
                    xj = [xs[:, b, bass.ds(j * QC, QC)] for b in range(2)]
                    dj = d3T[:, bass.ds(j * QC, QC)]

                    def up(e, b, hi, lo, dst, signal):
                        cols = slice(HID * e, HID * e + HID)
                        pe.matmul(dst, hi[:, cols], xj[b], start=True, stop=False)
                        pe.matmul(dst, lo[:, cols], xj[b], start=False, stop=True).then_inc(signal, 1)

                    def down(e):
                        pe.wait_ge(hid_v, step0 + 2 * e + 4)
                        pe.wait_ge(mix_v, expert0 + e + 1)
                        for b in range(2):
                            mm = pe.matmul(bank[4 + e % 2][64 * b:64 * b + 64, 0:QC], w3[:, e, :],
                                           hidT[(2 * e + b) % 4], start=True, stop=True)
                        mm.then_inc(down_p, 1)

                    for e in range(NE):
                        for b in range(2):
                            pe.wait_ge(silu_a, step0 + 2 * e + b + 1)
                            up(e, b, w1h, w1l, bank[b][:, 0:QC], h1_p)
                        pe.wait_ge(dw_a, expert0 + e + 1)
                        pe.matmul(bank[6 + e % 2][:, 0:QC], dsel[:, e, :], dj, start=True, stop=True).then_inc(dw_p, 1)
                        for b in range(2):
                            pe.wait_ge(hid_v, step0 + 2 * e + b + 1)
                            up(e, b, w2h, w2l, bank[2 + b][:, 0:QC], h2_p)
                        if e:
                            down(e - 1)
                    down(NE - 1)

            pe.wait_ge(params_in, PARAMS)
            pe.wait_ge(setup_v, SETUP_V)
            with pe.Fori(0, GROUPS) as g:
                wait_alone(pe, mix_v, g * FCH * NE + 2)
                for l in range(S):
                    scan_layer(g, l)
                attention(g)
                experts(g)

        @block.scalar
        def _(act):
            for i in range(S):
                act.sem_inc(evac[i], 2)
                act.sem_inc(seld[i], 1)
                act.sem_inc(decay[i], 2)
            act.sem_inc(qt_a, 2)
            act.sem_inc(silu_a, 2)
            act.sem_inc(dw_a, 2)

            def scan_layer(g, l):
                n, w, U = NC[l], CW[l], KU[l]
                act.preload_act_table_set("natural_log_exp_and_others")
                with act.Fori(0, n // 2) as i:
                    for k in range(2):
                        c = i * 2 + k
                        act.wait_ge(projz[l], g * n + c + 1)
                        act.wait_ge(corr[l], g * n + c + 1)
                        act.activation(eT[k][:, 0:w], bank[4 + k][:, 0:w], ACT.Abs, bias=bdt[:, l:l + 1])\
                            .then_inc(absd[l], 1)
                        wait_alone(act, proj[l], g * n + c + 1)
                        act.activation(col(Bn, c, w), bank[k][:, 0:w], ACT.Copy)
                        act.wait_ge(absd[l], g * n + c + 1)
                        act.wait_ge(dlt[l], g * n + c + 1)
                        act.activation(eT[k][:, 0:w], eT[k][:, 0:w], ACT.Exp, scale=-1.0).then_inc(expd[l], 1)
                        act.activation(col(Cn, c, w), bank[2 + k][:, 0:w], ACT.Copy).then_inc(evac[l], 1)
                        act.wait_ge(expd[l], g * n + c + 1)
                        act.activation(lT[k][:, 0:w], eT[k][:, 0:w], ACT.Ln, bias=1.0).then_inc(lnd[l], 1)
                act.wait_ge(dec_v[l], g * DECV + DECV)
                wait_alone(act, y0[l], g * U + U)

                def work(s, j):
                    wait_alone(act, bcast[l], (g * NS + s) * U + U)
                    act.activation(sel[j], blocks[:, :], ACT.Copy, scale=onehot[:, bass.ds(s, 1)]).then_inc(seld[l], 1)
                    with act.Fori(0, U // 2) as i:
                        for k in range(2):
                            q = i * 2 + k
                            wait_alone(act, scan[l], ((g * NS + s) * U + q + 1) * STEP[l])
                            act.activation(dA[k][:, 0:2 * w], col(delta, q, 2 * w), ACT.Exp,
                                           scale=Aslot[:, bass.ds(s, 1)]).then_inc(decay[l], 1)

                def skip(s, m):
                    act.wait_ge(decay[l], (g * NS + s) * U + 2)
                    act.sem_inc(seld[l], m)
                    act.sem_inc(decay[l], m * U)

                over_slots(act, skip, work)

            def attention(g):
                def squares(r, m, src):
                    act.wait_ge(cen_p, g * LN + m + 1)
                    act.activation(sqT[r % 2], src[:, 0:QC], ACT.Square).then_inc(csq_a, 1)

                def deviation(r, m, src):
                    act.wait_ge(var_p, g * LN + m + 1)
                    act.activation(xn[m], src[:, 0:QC], ACT.Ln, bias=eps[:, :]).then_inc(dev_a, 1)
                    act.wait_ge(dev_a, (g * LN + m) * 2 + 1)
                    act.activation(xn[m], xn[m], ACT.Exp, scale=-0.5).then_inc(dev_a, 1)

                def qk_squares(r):
                    act.wait_ge(qkv_v, g * TILES + 4 * r + 8)
                    act.wait_ge(nrm_v, (g * Q + r - 1) * NRV + 1) if r else None
                    act.activation(sq.rearrange("p (u k c) -> p u k c", k=2, c=64),
                                   qkv[:, QU * r:QU * r + QU, 0:144].rearrange("p u (k c) -> p u k c", k=2)[:, :, :, 0:64],
                                   ACT.Square).then_inc(nrm_a, 1)

                def qk_norms(r):
                    act.wait_ge(nrm_v, (g * Q + r) * NRV + 2)
                    act.activation(norm[r], norm[r], ACT.Ln).then_inc(nrm_a, 1)
                    act.wait_ge(nrm_a, (g * Q + r) * NRA + 2)
                    act.activation(norm[r], norm[r], ACT.Exp, scale=-0.5).then_inc(nrm_a, 1)

                def linear(r):
                    act.wait_ge(nrm_v, (g * Q + r) * NRV + NRV)
                    act.wait_ge(ones_g, g + 1)
                    units = slice(QU * r, QU * r + QU)
                    act.wait_ge(qt_p, (g * NB + 2 * r - 2) * FTN) if r > 1 else None
                    act.activation(qF[r % 2][:, :, QUAD:FEATS], qkv[:, units, 0:72], ACT.Copy).then_inc(lin_a, 1)
                    act.wait_ge(kv_p, g * NB + 2 * r - 2) if r > 1 else None
                    act.activation(kF[r % 2][:, :, QUAD:FEATS], qkv[:, units, 72:144], ACT.Copy).then_inc(lin_a, 1)

                def q_features(n):
                    act.wait_ge(at_p, g * NB + n + 1)
                    for f in range(FTN):
                        t = FTN * n + f
                        act.wait_ge(qt_p, g * FTN * NB + t + 1)
                        act.activation(qT[n % 2][:, f, :], bank[2 + t % 2][0:FT, 0:QC], ACT.Copy).then_inc(qt_a, 1)

                def reciprocal(n):
                    r = n // 2
                    act.wait_ge(pr_p, g * Q + r - 1) if r > 1 else None
                    act.wait_ge(at_p, g * NB + n + 3)
                    dst = attT[r % 2][:, TOK * (n % 2):TOK * (n % 2) + TOK]
                    act.activation(dst, bank[4 + n % 2][:, TOK:2 * TOK], ACT.Ln).then_inc(rec_a, 1)
                    act.wait_ge(rec_a, (g * NB + n) * 2 + 1)
                    act.activation(dst, dst, ACT.Exp, scale=-1.0).then_inc(rec_a, 1)

                def high(r, b, src):
                    act.wait_ge(dup_p, (g * Q + r) * 2 + b + 1)
                    act.activation(xs[:, b, QC * r:QC * r + QC], src[:, 0:QC], ACT.Copy).then_inc(hi_a, 1)

                def dispatch_transposed(r):
                    act.wait_ge(dt_p, g * Q + r + 1)
                    act.activation(d3T[:, QC * r:QC * r + QC], dispatchT, ACT.Copy)\
                        .then_inc(dt_a, 1)

                for r in range(0, Q, 2):
                    for i in (r, r + 1):
                        squares(i, i, bank[4 + i % 2])
                    if r:
                        qk_squares(0)
                    for i in (r, r + 1):
                        deviation(i, i, bank[6 + i % 2])
                qk_norms(0)
                qk_squares(1)
                linear(0)
                qk_norms(1)
                q_features(0)
                linear(1)
                qk_squares(2)
                for n in range(NB + 2):
                    r, odd = divmod(n - 2, 2)
                    if r >= 0 and odd:
                        high(r, 0, bank[7])
                    if n + 1 < NB:
                        q_features(n + 1)
                    if n == 0:
                        qk_norms(2)
                    if r >= 0 and not odd:
                        squares(r, Q + r, bank[7])
                    elif r >= 0:
                        act.wait_ge(gt_v, (g * Q + r) * GTN + 1)
                        dispatch_transposed(r - 1) if r else None
                        high(r, 1, bank[6])
                        act.wait_ge(gt_v, (g * Q + r) * GTN + 3)
                        act.activation(ex, lg, ACT.Exp).then_inc(gt_a, 1)
                    if n < NB:
                        reciprocal(n)
                    if n == 0:
                        qk_squares(3)
                    if n == 1:
                        qk_norms(3)
                        linear(2)
                    if n == 3:
                        linear(3)
                    if r >= 0 and not odd:
                        deviation(r, Q + r, bank[6])
                dispatch_transposed(Q - 1)

            def experts(g):
                act.preload_act_table(ACT.Silu)
                with act.Fori(0, FCH) as j:
                    step0 = (g * FCH + j) * FF
                    for i in range(FF):
                        act.wait_ge(h1_p, step0 + i + 1)
                        act.wait_ge(hid_v, step0 + i + 1)
                        act.activation(sT[i % 2], bank[i % 2][:, 0:QC], ACT.Silu).then_inc(silu_a, 1)
                        if i % 2:
                            e = i // 2
                            act.wait_ge(dw_p, (g * FCH + j) * NE + e + 1)
                            act.wait_ge(mix_v, (g * FCH + j) * NE + e + 1)
                            act.activation(wT[e % 2], bank[6 + e % 2][:, 0:QC], ACT.Copy).then_inc(dw_a, 1)

            act.wait_ge(zeroed, 1)
            for dst, src in first:
                act.dma_start(dst, src).then_inc(params_in, 16)
            act.wait_ge(params_in, PARAMS)
            act.wait_ge(setup_v, 1)
            act.activation(A[:, :, :], A[:, :, :], ACT.Exp).then_inc(setup_a, 1)
            act.activation(AT[:, :, :], AT[:, :, :], ACT.Exp).then_inc(setup_a, 1)
            with act.Fori(0, GROUPS) as g:
                for l in range(S):
                    scan_layer(g, l)
                attention(g)
                experts(g)

        @block.vector
        def _(v):
            for i in range(S):
                v.sem_inc(dlt[i], 2)
                v.sem_inc(relud[i], 2)
                v.sem_inc(corr[i], 2)
                v.sem_inc(ug[i], 2)
                v.sem_inc(scan[i], 2 * STEP[i])
                v.sem_inc(hc[i], 2)
            v.sem_inc(qkv_v, 4)
            v.sem_inc(kv_v, 2)
            v.sem_inc(att_v, 2)
            v.sem_inc(hid_v, 2)
            v.sem_inc(mix_v, 2)

            def setup():
                v.memset(wB[:, :, :], 0.0)
                v.memset(wC[:, :, :], 0.0).then_inc(zeroed, 1)
                v.memset(wqkv[:, :], 0.0)
                v.memset(gatew[:, :], 0.0)
                v.memset(wproj[:, :], 0.0).then_inc(zeroed, 1)
                v.memset(wZ[:, :, :], 0.0)
                v.memset(resid[:, :], 0.0)
                v.memset(ones64[:, :], 1.0)
                v.memset(eps[:, :], LN_EPS)
                v.memset(fscale[:, 8:16], SCALE).then_inc(zeroed, 1)
                v.wait_ge(zeroed, 3)
                v.wait_ge(params_in, PARAMS)
                v.tensor_scalar(A[:, :, :], A[:, :, :], 88.0, None, ALU.min)
                v.tensor_scalar(AT[:, :, :], AT[:, :, :], 88.0, None, ALU.min).then_inc(setup_v, 1)
                v.tensor_scalar(wC[:, 0:2, :], wC[:, 0:2, :], 0.5, None, ALU.mult)
                v.tensor_scalar(dskip[:, 0:2], dskip[:, 0:2], 0.5, None, ALU.mult)
                v.tensor_scalar(fscale[:, 0:8], temp, SCALE, None, ALU.mult)
                v.tensor_copy(identb[:, :], ident[:, :])
                for l in range(S):
                    for k in range(2):
                        blk = slice(64 * k, 64 * k + 64)
                        v.tensor_scalar(wZ[blk, l, blk], wdt[blk, l, :], w0[blk, l:l + 1], None, ALU.mult)
                v.wait_ge(setup_a, 2)
                v.tensor_scalar(A[:, :, :], A[:, :, :], -1.0, None, ALU.mult)
                v.tensor_scalar(AT[:, :, :], AT[:, :, :], -1.0, None, ALU.mult).then_inc(setup_v, 1)

            def split_experts():
                v.wait_ge(staged, 80)
                for b in range(2):
                    v.tensor_copy(dsel[:, :, 64 * b:64 * b + 64],
                                  bc(x0[0:96, 4096 + NE * b:4096 + NE * b + NE], 64))
                v.tensor_copy(w1h[:, :], x0[:, 0:2048])
                v.tensor_copy(w2h[:, :], x0[:, 2048:4096]).then_inc(split_v, 1)
                v.wait_ge(split_v, 1)
                v.tensor_tensor(w1l[:, :], x0[:, 0:2048], w1h[:, :].bitcast(F32), ALU.subtract)
                v.tensor_tensor(w2l[:, :], x0[:, 2048:4096], w2h[:, :].bitcast(F32), ALU.subtract).then_inc(split_v, 1)

            def scan_layer(g, l):
                n, w, U, x = NC[l], CW[l], KU[l], xl[l]
                def relu(c, k):
                    v.wait_ge(absd[l], g * n + c + 1)
                    v.tensor_scalar(rT[k][:, 0:w], bank[4 + k][:, 0:w], bdt[:, l:l + 1], 0.0, ALU.add, ALU.max)\
                        .then_inc(relud[l], 1)

                def softplus(c, k, more):
                    v.wait_ge(onep[l], g * n + c + 1)
                    e, t = eT[k][:, 0:w], uT[k][:, 0:w]
                    v.scalar_tensor_tensor(t, t, 1.0, e, ALU.subtract, ALU.subtract, reverse1=True)\
                        .then_inc(corr[l], 1)
                    if more:
                        relu(c + 1, 1 - k)
                    v.wait_ge(corr[l], g * n + c + 3)
                    v.wait_ge(wsum[l], g * n + c + 1)
                    v.tensor_tensor(col(delta, c, w), t, lT[k][:, 0:w], ALU.add).then_inc(dlt[l], 1)
                    v.wait_ge(dlt[l], g * n + c + 3)
                    v.tensor_reduce(mins[:, bass.ds(c, 1)], col(delta, c, w), AXX, ALU.min)
                    v.tensor_tensor(col(u, c, w), col(delta, c, w), col(x, c, w), ALU.mult).then_inc(udone[l], 1)

                relu(0, 0)
                with v.Fori(0, n // 2 - 1) as i:
                    for k in range(2):
                        softplus(i * 2 + k, k, True)
                softplus(n - 2, 0, True)
                softplus(n - 1, 1, False)

                step = [0]

                def then(ins, last=True):
                    if last:
                        step[0] += 1
                        ins.then_inc(dec_v[l], 1)
                        v.wait_ge(dec_v[l], g * DECV + step[0])

                v.wait_ge(udone[l], g * n + n)
                then(v.tensor_reduce(minall[:, :], mins[:, 0:n], AXX, ALU.min))
                v.tensor_scalar(amax2[:, 0, :], A[:, l, :], minall[:, :], None, ALU.mult)
                then(v.tensor_scalar(amax2[:, 1, :], A[:, l, :], minall[:, :], None, ALU.mult))
                v.wait_ge(dec_p[l], g * DECP + 1)
                then(v.tensor_reduce(amx[:, :], bank[6][:, 0:128], AXX, ALU.max))
                v.tensor_scalar(slow[:, :], amx[:, :], EXP_ZERO, None, ALU.is_gt)
                then(v.tensor_scalar(fast[:, :], amx[:, :], EXP_ZERO, None, ALU.is_le))
                then(v.tensor_scalar(fastblk[:, :], blocks[:, :], fast[:, :], None, ALU.mult))
                v.wait_ge(dec_p[l], g * DECP + 2)
                v.tensor_copy(rank[:, :], bank[6][:, 128:129])
                then(v.tensor_copy(count[:, :], bank[6][0:1, 130:131]))
                then(v.tensor_scalar(onehot[:, :], slotno[:, :], rank[:, :], slow[:, :], ALU.is_equal, ALU.mult))
                v.wait_ge(dec_p[l], g * DECP + 3)
                v.tensor_copy(Aslot[:, :], bank[6][:, 256:256 + NS]).then_inc(dec_v[l], 1)
                assert step[0] == DECV - 1

                with v.Fori(0, U // 2) as i:
                    for k in range(2):
                        q = i * 2 + k
                        v.wait_ge(gsum[l], g * U + q + 3)
                        v.tensor_tensor(gT[k][:, 0:2 * w].rearrange("p (b t) -> p b t", b=2), pairs[2 + k][:, :, 0:w],
                                        col(u, q, 2 * w).rearrange("p (b t) -> p b t", b=2), ALU.mult).then_inc(ug[l], 1)
                        v.wait_ge(ug[l], g * U + q + 3)
                        y = col(x, q, 2 * w)
                        v.scalar_tensor_tensor(y, y, dskip[:, l:l + 1], gT[k][:, 0:2 * w], ALU.mult, ALU.add)\
                            .then_inc(y0[l], 1)

                def work(s, j):
                    with v.Fori(0, U // 2) as i:
                        for k in range(2):
                            q = i * 2 + k
                            unit = (g * NS + s) * U + q
                            h = hT[k]
                            v.wait_ge(bcast[l], unit + 1 + 2 * U)
                            bu = pairs[k][:, :, 0:w]
                            v.tensor_tensor(bu, bu, col(u, q, 2 * w).rearrange("p (b t) -> p b t", b=2), ALU.mult)\
                                .then_inc(scan[l], 1)
                            v.wait_ge(decay[l], unit + 3)
                            v.wait_ge(ysum[l], unit + 1)
                            parts = STEP[l] - 1
                            m = 2 * w // parts
                            for p in range(parts):
                                v.wait_ge(scan[l], (unit + 2) * STEP[l] + (1 + p if l == 0 else 1))
                                b, off = divmod(p * m, w)
                                first = h[:, p * m - 1:p * m] if l == 0 and p else 0.0
                                v.tensor_tensor_scan(h[:, p * m:p * m + m], dA[k][:, p * m:p * m + m],
                                                     pairs[k][:, b, off:off + m], first, ALU.mult, ALU.add)\
                                    .then_inc(scan[l], 1)
                            v.wait_ge(scan[l], (unit + 3) * STEP[l])
                            h2 = h[:, 0:2 * w].rearrange("p (b t) -> p b t", b=2)
                            v.tensor_tensor(h2, h2, pairs[2 + k][:, :, 0:w], ALU.mult).then_inc(hc[l], 1)

                def skip(s, m):
                    v.wait_ge(hc[l], (g * NS + s) * U + 2)
                    v.sem_inc(scan[l], m * U * STEP[l])
                    v.sem_inc(hc[l], m * U)

                over_slots(v, skip, work)
                v.wait_ge(ysum[l], (g + 1) * NS * U + 2)
                v.wait_ge(y0[l], g * U + U)
                if l < S - 1:
                    L2 = LEN[l + 1]
                    y = x.rearrange("p (b t) -> p b t", b=NB)[:, :, 0:2 * L2].rearrange("p b (t k) -> p b t k", k=2)
                    for b in range(0, NB, NB // PARTS):
                        items = slice(b, b + NB // PARTS)
                        v.tensor_tensor(xl[l + 1].rearrange("p (b t) -> p b t", b=NB)[:, items],
                                        y[:, items, :, 0], y[:, items, :, 1], ALU.add).then_inc(pooled, 1)
                else:
                    v.wait_ge(out_d, g * FCH * 16 + 16)
                    v.tensor_copy(resid[:, :].rearrange("p (b t) -> p b t", b=NB)[:, :, 0:NT],
                                  x.rearrange("p (b t) -> p b t", b=NB)).then_inc(pooled, 1)

            def bc(t, m):
                return t.unsqueeze(len(t.shape)).to_broadcast(list(t.shape) + [m])

            def over(t, m, at):
                shape = list(t.shape)
                shape.insert(at, m)
                return t.unsqueeze(at).to_broadcast(shape)

            def attention(g):
                def normalize(r, m, src):
                    v.wait_ge(dev_a, (g * LN + m) * 2 + 2)
                    v.tensor_tensor(xn[m], src[:, 0:QC], xn[m], ALU.mult).then_inc(xn_v, 1)

                def qkv_bias(r):
                    for i in range(4 * r, 4 * r + 4):
                        v.wait_ge(qkv_p, g * TILES + i + 1)
                        dst = qkv[:, 2 * i:2 * i + 2, :].rearrange("p b (k c) -> p b k c", c=72)[:, :, :, 0:64]
                        v.tensor_tensor(dst, bank[i % 4][0:TP, 0:384].rearrange("p (b k c) -> p b k c", b=2, k=3),
                                        bqkv[0:TP, :].rearrange("p (b k c) -> p b k c", b=2, k=3), ALU.add)\
                            .then_inc(qkv_v, 1)

                def norm_step(r, i, ins):
                    ins.then_inc(nrm_v, 1)
                    v.wait_ge(nrm_v, (g * Q + r) * NRV + i)

                def qk_sums(r):
                    v.wait_ge(nrm_a, (g * Q + r) * NRA + 1)
                    norm_step(r, 1, v.tensor_reduce(norm[r].rearrange("p u h -> p (u h)"),
                                                    sq.rearrange("p (n d) -> p n d", d=D), AXX, ALU.add))
                    norm_step(r, 2, v.tensor_tensor(norm[r], norm[r], over(floor[0:TP, :], QU, 1), ALU.max))

                def heads(r, at):
                    return qkv[:, QU * r:QU * r + QU, at:at + 64].rearrange("p u (h d) -> p u h d", d=D)

                def qk_scale(r):
                    v.wait_ge(nrm_a, (g * Q + r) * NRA + 3)
                    norm_step(r, 3, v.tensor_tensor(norm[r], norm[r], over(fscale[0:TP, :], QU, 1), ALU.mult))
                    norm_step(r, 4, v.tensor_tensor(heads(r, 72), heads(r, 72), bc(norm[r][:, :, 8:16], D), ALU.mult))
                    norm_step(r, 5, v.tensor_tensor(heads(r, 0), heads(r, 0), bc(norm[r][:, :, 0:8], D), ALU.mult))

                def q_products(r):
                    v.wait_ge(qt_p, (g * NB + 2 * r - 2) * FTN) if r > 1 else None
                    products(v, qF[r % 2], heads(r, 0)).then_inc(qf_v, 1)

                def moments(n):
                    v.wait_ge(kv_p, g * NB + n + 1)
                    v.wait_ge(at_p, g * NB + n + 1)
                    src = bank[n % 2][0:FT, 0:2 * FTN * 65].rearrange("p (f c) -> p f c", c=65)
                    v.tensor_tensor(kvm[n % 2][:, 0], src[:, :, 1:65], featw[:, :, :], ALU.mult)
                    v.tensor_tensor(kvm[n % 2][:, 1], src[:, :, 0:1].to_broadcast([FT, 2 * FTN, 64]), featw[:, :, :],
                                    ALU.mult).then_inc(kv_v, 1)

                def attend(n):
                    v.wait_ge(rec_a, (g * NB + n) * 2 + 2)
                    dst = attT[n // 2 % 2][:, TOK * (n % 2):TOK * (n % 2) + TOK]
                    v.tensor_tensor(dst, bank[4 + n % 2][:, 0:TOK], dst, ALU.mult).then_inc(att_v, 1)

                def low(r, b, src):
                    v.wait_ge(hi_a, (g * Q + r) * 2 + b + 1)
                    dst = xs[64:128, b, QC * r:QC * r + QC]
                    v.tensor_tensor(dst, src[64:128, 0:QC], dst.bitcast(F32), ALU.subtract).then_inc(lo_v, 1)

                v.wait_ge(later_in, LATER)
                normalize(0, 0, bank[4])
                normalize(1, 1, bank[5])
                qkv_bias(0)
                qkv_bias(1)
                qk_sums(0)
                normalize(2, 2, bank[4])
                normalize(3, 3, bank[5])
                qk_scale(0)
                qkv_bias(2)
                qk_sums(1)
                qkv_bias(3)
                qk_scale(1)
                q_products(0)
                moments(0)
                q_products(1)
                for n in range(NB + 2):
                    r, odd = divmod(n - 2, 2)
                    if n + 1 < NB:
                        moments(n + 1)
                    if n < 2:
                        qk_sums(2 + n)
                    if r >= 0 and not odd:
                        v.wait_ge(pr_p, g * Q + r + 1)
                        x = resid[:, QC * r:QC * r + QC]
                        v.scalar_tensor_tensor(x, bank[6][:, 0:QC], bproj[:, :], x, ALU.add, ALU.add).then_inc(pr_v, 1)
                    elif r >= 0:
                        finish = gating(g, r)
                        low(r, 0, bank[7])
                        low(r, 1, bank[6])
                    if n < NB:
                        attend(n)
                    if n == 0:
                        qk_scale(2)
                    if n == 1:
                        q_products(2)
                    if n == 2:
                        qk_scale(3)
                    if r >= 0 and not odd:
                        normalize(r, Q + r, bank[7])
                    elif r >= 0:
                        finish()
                    if n == 4:
                        q_products(3)

            def gating(g, r):
                step = [0]

                def then(ins):
                    step[0] += 1
                    ins.then_inc(gt_v, 1)
                    v.wait_ge(gt_v, (g * Q + r) * GTN + step[0])

                m1, first, m2, den = (small[:, k, :] for k in range(4))
                d = d3[:, r % 2]
                v.wait_ge(gt_p, g * Q + r + 1)
                then(v.tensor_tensor(lg, bank[6][0:TP, 0:QU * NE].rearrange("p (u e) -> p u e", e=NE),
                                     over(gateb[0:TP, :], QU, 1), ALU.add))
                then(v.tensor_reduce(m1, lg, AXX, ALU.max))

                def first_of(dst):
                    then(v.tensor_reduce(first, eq, AXX, ALU.max))
                    then(v.tensor_tensor(dst, eq, bc(first, NE), ALU.is_equal))

                then(v.tensor_tensor(lg, lg, bc(m1, NE), ALU.subtract))
                then(v.scalar_tensor_tensor(eq, lg, 0.0, over(ridx[0:TP, :], QU, 1), ALU.is_equal, ALU.mult))
                first_of(mask)
                then(v.scalar_tensor_tensor(rest, mask, BIG_NEG, lg, ALU.mult, ALU.add))
                then(v.tensor_reduce(m2, rest, AXX, ALU.max))
                then(v.tensor_tensor(eq, rest, bc(m2, NE), ALU.is_equal))
                then(v.tensor_tensor(eq, eq, over(ridx[0:TP, :], QU, 1), ALU.mult))
                first_of(mask2)

                def finish():
                    v.wait_ge(gt_a, g * Q + r + 1)
                    then(v.tensor_tensor(mask, mask, mask2, ALU.add))
                    then(v.tensor_tensor(lg, ex, mask, ALU.mult))
                    then(v.tensor_reduce(den, lg, AXX, ALU.add))
                    then(v.reciprocal(den, den))
                    then(v.tensor_tensor(lg, lg, bc(den, NE), ALU.mult))
                    then(v.tensor_copy(d[:, :, 0:16], lg))
                    then(v.tensor_tensor(lg, lg, d[:, :, 0:16], ALU.subtract))
                    then(v.tensor_copy(d[:, :, 16:32], lg))
                    then(v.tensor_tensor(lg, lg, d[:, :, 16:32], ALU.subtract))
                    v.tensor_copy(d[:, :, 32:48], lg).then_inc(gt_v, 1)
                    assert step[0] == GTN - 1

                return finish

            def experts(g):
                with v.Fori(0, FCH) as j:
                    step0 = (g * FCH + j) * FF
                    expert0 = (g * FCH + j) * NE

                    def mix(e):
                        v.wait_ge(down_p, expert0 + e + 3)
                        v.wait_ge(dw_a, expert0 + e + 3)
                        v.wait_ge(add_g, expert0 + e + 1)
                        v.tensor_tensor(mT[e % 2], bank[4 + e % 2][:, 0:QC], wT[e % 2], ALU.mult)\
                            .then_inc(mix_v, 1)

                    for e in range(NE):
                        for b in range(2):
                            i = 2 * e + b
                            v.wait_ge(silu_a, step0 + i + 3)
                            v.wait_ge(h2_p, step0 + i + 1)
                            v.wait_ge(down_p, expert0 + e + 1)
                            v.tensor_tensor(hidT[i % 4], bank[2 + b][:, 0:QC], sT[b], ALU.mult).then_inc(hid_v, 1)
                        if e:
                            mix(e - 1)
                    mix(NE - 1)

            setup()
            with v.Fori(0, GROUPS) as g:
                for l in range(S):
                    scan_layer(g, l)
                    if l == 1:
                        with v.If(g < 1):
                            split_experts()
                        with v.Else():
                            v.nop()
                attention(g)
                experts(g)

        @block.gpsimd
        def _(pool):
            for i in range(S):
                pool.sem_inc(ysum[i], 2)
            pool.sem_inc(add_g, 2)

            def scan_layer(g, l):
                n, w, U, x = NC[l], CW[l], KU[l], xl[l]
                with pool.Fori(0, n // 2) as i:
                    for k in range(2):
                        c = i * 2 + k
                        wait_alone(pool, expd[l], g * n + c + 1)
                        pool.tensor_scalar(uT[k][:, 0:w], eT[k][:, 0:w], 1.0, 1.0, ALU.mult, ALU.add).then_inc(onep[l], 1)
                        pool.wait_ge(relud[l], g * n + c + 3)
                        pool.wait_ge(lnd[l], g * n + c + 1)
                        pool.tensor_tensor(lT[k][:, 0:w], lT[k][:, 0:w], rT[k][:, 0:w], ALU.add).then_inc(wsum[l], 1)
                wait_alone(pool, dlt[l], g * n + n + 2)
                with pool.Fori(0, U // 2) as i:
                    for k in range(2):
                        q = i * 2 + k
                        pool.wait_ge(gsum[l], g * U + q + 1)
                        pool.tensor_tensor(bcT[k][:, 0:2 * w], col(Bn, q, 2 * w), col(Cn, q, 2 * w), ALU.mult)\
                            .then_inc(bcd[l], 1)
                wait_alone(pool, dec_v[l], g * DECV + DECV)

                def work(s, j):
                    with pool.Fori(0, U // 2) as i:
                        for k in range(2):
                            q = i * 2 + k
                            unit = (g * NS + s) * U + q
                            pool.wait_ge(hc[l], unit + 3)
                            pool.wait_ge(ysum[l], unit + 2)
                            y = col(x, q, 2 * w)
                            pool.tensor_tensor(y, y, hT[k][:, 0:2 * w], ALU.add).then_inc(ysum[l], 1)

                def skip(s, m):
                    pool.wait_ge(ysum[l], (g * NS + s) * U + 2)
                    pool.sem_inc(ysum[l], m * U)

                over_slots(pool, skip, work)

            def attention(g):
                wait_alone(pool, pooled, g * POOLED + POOLED)
                pool.memset(qkv[:, :, 64:72], 1.0)
                pool.memset(qkv[:, :, 136:144], 1.0).then_inc(ones_g, 1)
                for r in range(Q):
                    k4 = qkv[:, QU * r:QU * r + QU, 72:136].rearrange("p u (h d) -> p u h d", d=D)
                    pool.wait_ge(nrm_v, (g * Q + r) * NRV + 4)
                    if r > 1:
                        pool.wait_ge(kv_p, g * NB + 2 * r - 2)
                    products(pool, kF[r % 2], k4).then_inc(kf_g, 1)

            with pool.Fori(0, GROUPS) as g:
                for l in range(S):
                    scan_layer(g, l)
                attention(g)
                with pool.Fori(0, FCH) as j:
                    expert0 = (g * FCH + j) * NE
                    for e in range(NE):
                        pool.wait_ge(add_g, expert0 + e + 2)
                        wait_alone(pool, mix_v, expert0 + e + 3)
                        r = col(resid, j, QC)
                        pool.tensor_tensor(r, r, mT[e % 2], ALU.add).then_inc(add_g, 1)


def products(eng, dst, t):
    at = 0
    for k in range(D):
        m = D - k
        ins = eng.tensor_tensor(dst[:, :, at:at + H * m].rearrange("p u (h d) -> p u h d", d=m),
                                t[:, :, :, 0:m], t[:, :, :, k:D], ALU.mult)
        at += H * m
    return ins



def shape_constants():
    import numpy as np
    f = np.float32
    half = np.arange(128) // 64
    featw = np.zeros((FEATS, 64), f)
    scale2 = D ** 0.5

    def put(row, head, weight):
        featw[row, 8 * head:8 * head + 8] = weight

    row = 0
    for k in range(D):
        for head in range(H):
            for _ in range(D - k):
                put(row, head, 0.5 if k == 0 else 1.0)
                row += 1
    for i in range(64):
        put(QUAD + i, i // D, scale2)
    for head in range(H):
        put(QUAD + 64 + head, head, scale2 * scale2)
    dsel = np.zeros((2, 3, NE, 2 * NE), f)
    for b in range(2):
        for e in range(NE):
            dsel[b, :, e, NE * b + e] = 1
    n = np.arange(64)
    tri = np.zeros((128, 128), f)
    tri[:64] = np.tile((n[:, None] < n[None, :]).astype(f), (1, 2))
    return {
        "ident": np.eye(128, dtype=f), "blocks": (half[:, None] == half[None, :]).astype(f), "tri": tri,
        "slotno": np.tile(np.arange(NS, dtype=f), (128, 1)), "ridx": np.tile(np.arange(NE, 0, -1, dtype=f), (128, 1)),
        "featw": np.tile(featw.reshape(FTN, FT, 64).transpose(1, 0, 2), (1, 2, 1)),
        "dsel": dsel.reshape(6 * NE, 2 * NE),
        "floor": np.tile(np.array([NORM_EPS ** 2 / D ** 0.5] * 8 + [NORM_EPS ** 2] * 8, f), (128, 1)),
        "averaging": (half[:, None] == half[None, :]).astype(f) / 64,
        "centering": np.eye(128, dtype=f) - (half[:, None] == half[None, :]).astype(f) / 64,
    }


def laid_out(i):
    import numpy as np
    i = {k: np.asarray(x) for k, x in i.items()}

    def rows(x, n=128):
        return np.tile(x.reshape(1, -1), (n, 1))

    x = i["x"].reshape(2, 16, SEQ, C).transpose(0, 3, 1, 2)
    w = i["L0_tok_W_dbc"].transpose(2, 0, 1)
    alog = i["L0_tok_A_log"]
    a = {
        "x": x.reshape(128, GROUPS, NB * SEQ),
        "w_tok": w,
        "alogT": np.tile(alog.transpose(2, 0, 1), (1, 1, 2)),
        "wqkv": i["L0_attn_Wqkv"].T, "bqkv": rows(np.tile(i["L0_attn_bqkv"], 2)),
        "wproj": i["L0_attn_Wproj"].T, "bproj": np.tile(i["L0_attn_bproj"][:, None], (2, 1)),
        "gate_w": i["L0_ffn_gate_w"], "gate_b": rows(i["L0_ffn_gate_b"]),
        "w1": i["L0_ffn_w1"].transpose(1, 0, 2).reshape(64, NE * HID),
        "w2": i["L0_ffn_w2"].transpose(1, 0, 2).reshape(64, NE * HID),
        "w3": i["L0_ffn_w3"].transpose(1, 0, 2),
    }
    c = shape_constants()
    a["packed"] = np.concatenate([c.pop(k) for k in ("ident", "blocks", "tri", "slotno")] + [
        rows(i["L0_attn_temperature"])] + [np.tile(t, (2, 1)) for t in (
            w[:, :, 0], i["L0_tok_b_dt"].T, i["L0_tok_D"].T)] + [
        rows(i["L0_tok_W_dt"]), np.tile(alog.transpose(1, 0, 2).reshape(64, LAYERS * NS), (2, 1))], axis=1)
    return {k: np.ascontiguousarray(x) for k, x in (a | c).items()}


def kernel(**inputs):
    import numpy as np
    import concourse.bacc as bacc
    from concourse.bass_utils import run_bass_kernel_spmd

    nc = bacc.Bacc("TRN2", target_bir_lowering=False, num_devices=1)
    arrays = {f"in_{k}": x for k, x in laid_out(inputs).items()}
    a = {k[3:]: nc.dram_tensor(k, x.shape, mybir.dt.from_np(x.dtype), kind="ExternalInput").ap()
         for k, x in arrays.items()}
    out = nc.dram_tensor("out", (128, 16, NT), F32, kind="ExternalOutput").ap()
    program(nc, a, out)
    r = run_bass_kernel_spmd(nc, [arrays], core_ids=[0])
    y = np.asarray(r.results[0]["out"]).reshape(2, C, 16, NT)
    return np.ascontiguousarray(y.transpose(0, 2, 3, 1)).reshape(BATCH, NT, C)
```
